# Optimizing a Trainium2 kernel written in Bass

```python
import numpy as np
import jax
import jax.numpy as jnp

def _softmax(x, axis=-1):
    return jax.nn.softmax(x, axis=axis)

def _gelu(x):
    return jax.nn.gelu(x, approximate=True)

def _silu(x):
    return jax.nn.silu(x)

def _sigmoid(x):
    return jax.nn.sigmoid(x)

def _layernorm(x, axis=-1, eps=1e-05):
    m = jnp.mean(x, axis=axis, keepdims=True)
    v = jnp.var(x, axis=axis, keepdims=True)
    return (x - m) / jnp.sqrt(v + eps)

def _scatter_add(tgt, idx, src, axis=0):
    return tgt.at[idx].add(src)

def _segment_sum(src, seg, n):
    return jax.ops.segment_sum(src, seg, n)
kernel_name = 'mk_adj_preln_d2_adj_r2_aa3cb6'

def setup_inputs(seed: int=0):
    np.random.seed(seed)
    _w = jnp.asarray

    def _rec_inputs():
        import jax
        import jax.numpy as jnp
        _gk = jax.random.key(seed)
        x = -0.0003929 + 0.9999 * jax.random.normal(jax.random.fold_in(_gk, 1), (128, 128, 128), jnp.float32)
        _w = (1.0 + jnp.arange(128, dtype=jnp.float32)) ** (-0.5)
        _w = _w / _w.mean()
        _pij = jnp.clip(0.125 * _w[:, None] * _w[None, :], 0.0, 1.0)
        _a = jax.random.uniform(jax.random.fold_in(_gk, 2), (128, 128)) < _pij
        _a = jnp.logical_or(_a, jnp.swapaxes(_a, -1, -2))
        _a = jnp.logical_or(_a, jnp.eye(128, dtype=bool))
        _af = _a.astype(jnp.float32)
        _d = jnp.maximum(_af.sum(-1), 1.0) ** (-0.5)
        _af = _af * _d[..., :, None] * _d[..., None, :]
        adj = _af
        return (x, adj)
    x, adj = _rec_inputs()

    def _L0_gnn_setup():
        import jax, jax.numpy as jnp
        import numpy as np
        B, N, D_IN, HID, D_OUT = (64, 512, 128, 128, 128)
        key = jax.random.key(seed)
        kf, ka, kw1, kw2 = jax.random.split(key, 4)
        features = jax.random.normal(kf, (B, N, D_IN), dtype=jnp.float32)
        A = jax.random.uniform(ka, (N, N), dtype=jnp.float32)
        A = 0.5 * (A + A.T)
        lim1 = float(np.sqrt(6.0 / (D_IN + HID)))
        lim2 = float(np.sqrt(6.0 / (HID + D_OUT)))
        W1 = jax.random.uniform(kw1, (D_IN, HID), minval=-lim1, maxval=lim1, dtype=jnp.float32)
        b1 = jnp.zeros((HID,), jnp.float32)
        W2 = jax.random.uniform(kw2, (HID, D_OUT), minval=-lim2, maxval=lim2, dtype=jnp.float32)
        b2 = jnp.zeros((D_OUT,), jnp.float32)
        return {'features': features, 'A': A, 'W1': W1, 'b1': b1, 'W2': W2, 'b2': b2}
    _L0_gnn_all = _L0_gnn_setup()
    _L0_gnn_in = {k: v for k, v in _L0_gnn_all.items() if k in ('W1', 'b1', 'W2', 'b2')}
    del _L0_gnn_all

    def _L1_gnn_setup():
        import jax, jax.numpy as jnp
        import numpy as np
        B, T, D, H = (64, 1024, 128, 128)
        MAX_SKIP = 4

        def _lstm_last(Wih, Whh, bih, bhh, xs):
            N, _, Hd = xs.shape
            bias = bih + bhh

            def step(carry, x_t):
                h, c = carry
                g = x_t @ Wih.T + h @ Whh.T + bias
                i, f, gg, o = jnp.split(g, 4, axis=-1)
                c = jax.nn.sigmoid(f) * c + jax.nn.sigmoid(i) * jnp.tanh(gg)
                h = jax.nn.sigmoid(o) * jnp.tanh(c)
                return ((h, c), None)
            init = (jnp.zeros((N, Hd), xs.dtype), jnp.zeros((N, Hd), xs.dtype))
            (h_last, _), _ = jax.lax.scan(step, init, jnp.swapaxes(xs, 0, 1))
            return h_last
        key = jax.random.key(seed)
        ks = jax.random.split(key, 8)
        s = 0.05
        x = jax.random.normal(ks[0], (B, T, D), jnp.float32)
        adj = jax.random.uniform(ks[1], (T, T), jnp.float32) / T
        Wg0 = jax.random.normal(ks[2], (D, H), jnp.float32) * s
        bg0 = jnp.zeros((H,), jnp.float32)
        Wg1 = jax.random.normal(ks[3], (H, H), jnp.float32) * s
        bg1 = jnp.zeros((H,), jnp.float32)
        Wih = jax.random.normal(ks[4], (MAX_SKIP, 4 * H, H), jnp.float32) * s
        Whh = jax.random.normal(ks[5], (MAX_SKIP, 4 * H, H), jnp.float32) * s
        bih = jax.random.normal(ks[6], (MAX_SKIP, 4 * H), jnp.float32) * s
        bhh = jax.random.normal(ks[7], (MAX_SKIP, 4 * H), jnp.float32) * s
        return dict(x=x, adj=adj, Wg0=Wg0, bg0=bg0, Wg1=Wg1, bg1=bg1, Wih=Wih, Whh=Whh, bih=bih, bhh=bhh)
    _L1_gnn_all = _L1_gnn_setup()
    _L1_gnn_in = {k: v for k, v in _L1_gnn_all.items() if k in ('Wg0', 'bg0', 'Wg1', 'bg1', 'Wih', 'Whh', 'bih', 'bhh')}
    del _L1_gnn_all
    return {'x': x, 'adj': adj, 'L0_gnn_W1': _L0_gnn_in['W1'], 'L0_gnn_b1': _L0_gnn_in['b1'], 'L0_gnn_W2': _L0_gnn_in['W2'], 'L0_gnn_b2': _L0_gnn_in['b2'], 'L1_gnn_Wg0': _L1_gnn_in['Wg0'], 'L1_gnn_bg0': _L1_gnn_in['bg0'], 'L1_gnn_Wg1': _L1_gnn_in['Wg1'], 'L1_gnn_bg1': _L1_gnn_in['bg1'], 'L1_gnn_Wih': _L1_gnn_in['Wih'], 'L1_gnn_Whh': _L1_gnn_in['Whh'], 'L1_gnn_bih': _L1_gnn_in['bih'], 'L1_gnn_bhh': _L1_gnn_in['bhh']}

def reference(x, adj, L0_gnn_W1, L0_gnn_b1, L0_gnn_W2, L0_gnn_b2, L1_gnn_Wg0, L1_gnn_bg0, L1_gnn_Wg1, L1_gnn_bg1, L1_gnn_Wih, L1_gnn_Whh, L1_gnn_bih, L1_gnn_bhh):
    import jax
    import jax.numpy as jnp

    def _L0_gnn_ref(features, A, W1, b1, W2, b2):
        import jax, jax.numpy as jnp
        import numpy as np
        B, N, D_IN, HID, D_OUT = (64, 512, 128, 128, 128)
        deg = jnp.sum(A, axis=0) + jnp.sum(A, axis=1) - jnp.diagonal(A)
        d_inv_sqrt = jnp.where(deg > 0, jax.lax.rsqrt(deg), 0.0)
        L = jnp.diag(deg) - A
        L_norm = d_inv_sqrt[:, None] * L * d_inv_sqrt[None, :]
        _, U = jnp.linalg.eigh(L_norm)
        agg = jnp.einsum('mn,bnd->bmd', U.T, features)
        h = jax.nn.relu(agg @ W1 + b1)
        out = h @ W2 + b2
        return jnp.einsum('nm,bmd->bnd', U, out)

    def _L1_gnn_ref(x, adj, Wg0, bg0, Wg1, bg1, Wih, Whh, bih, bhh):
        import jax, jax.numpy as jnp
        import numpy as np
        B, T, D, H = (64, 1024, 128, 128)
        MAX_SKIP = 4

        def _lstm_last(Wih, Whh, bih, bhh, xs):
            N, _, Hd = xs.shape
            bias = bih + bhh

            def step(carry, x_t):
                h, c = carry
                g = x_t @ Wih.T + h @ Whh.T + bias
                i, f, gg, o = jnp.split(g, 4, axis=-1)
                c = jax.nn.sigmoid(f) * c + jax.nn.sigmoid(i) * jnp.tanh(gg)
                h = jax.nn.sigmoid(o) * jnp.tanh(c)
                return ((h, c), None)
            init = (jnp.zeros((N, Hd), xs.dtype), jnp.zeros((N, Hd), xs.dtype))
            (h_last, _), _ = jax.lax.scan(step, init, jnp.swapaxes(xs, 0, 1))
            return h_last
        h = jax.nn.relu(jnp.einsum('ts,bsh->bth', adj, x @ Wg0 + bg0))
        h = jax.nn.relu(jnp.einsum('ts,bsh->bth', adj, h @ Wg1 + bg1))
        Bv, Tv, Hd = h.shape
        for p in range(1, MAX_SKIP + 1):
            nw = Tv // p
            wins = h[:, :nw * p, :].reshape(Bv * nw, p, Hd)
            last = _lstm_last(Wih[p - 1], Whh[p - 1], bih[p - 1], bhh[p - 1], wins)
            idx = jnp.arange(nw) * p + (p - 1)
            h = h.at[:, idx, :].set(last.reshape(Bv, nw, Hd))
        return h
    h = jnp.maximum(_layernorm(x, axis=-1), 0.0)
    x = x + _L0_gnn_ref(h, adj, L0_gnn_W1, L0_gnn_b1, L0_gnn_W2, L0_gnn_b2)
    h = jnp.maximum(_layernorm(x, axis=-1), 0.0)
    x = x + _L1_gnn_ref(h, adj, L1_gnn_Wg0, L1_gnn_bg0, L1_gnn_Wg1, L1_gnn_bg1, L1_gnn_Wih, L1_gnn_Whh, L1_gnn_bih, L1_gnn_bhh)
    return x

_drawn_inputs = setup_inputs


def setup_inputs(seed=0):
    import zlib

    import numpy as np

    out = dict(_drawn_inputs(seed))
    spreads = {'L0_gnn_b1': (0.0, 0.1),
     'L0_gnn_b2': (0.0, 0.1),
     'L1_gnn_bg0': (0.0, 0.8),
     'L1_gnn_bg1': (0.0, 0.8)}
    factors = {'L1_gnn_Wg0': 8.0,
     'L1_gnn_Wg1': 8.0,
     'L1_gnn_Wih': 8.0,
     'L1_gnn_Whh': 8.0,
     'L1_gnn_bih': 3.175,
     'L1_gnn_bhh': 3.223}
    for name, (base, spread) in spreads.items():
        noise = np.random.default_rng([zlib.crc32(name.encode()), seed]).standard_normal(out[name].shape)
        drawn = base * np.exp(spread * noise) if base else spread * noise
        out[name] = jnp.asarray(drawn.astype(out[name].dtype))
    for name, factor in factors.items():
        out[name] = (out[name] * factor).astype(out[name].dtype)
    return out
```

```python
from contextlib import ExitStack

import concourse.bass as bass
from concourse import mybir

F32 = mybir.dt.float32
ALU = mybir.AluOpType
ACT = mybir.ActivationFunctionType
AX_X = mybir.AxisListType.X

N = 128
F = 32
LEAF = 16
LEVELS = 4
SPLITS = [[64], [32, 96], [16, 48, 80, 112]]
LANES = 2 * LEVELS
QR_SWEEPS = 16
DEFLATE = 8.0 * 2.0 ** -24
QR_EPS2 = (2.0 ** -24) ** 2
TINY = 1e-30
QR_PER = 97
RAYLEIGH_CLIP = 1e-5
REGULAR = 1e-12
REFINES = 2

BATCH, D = 128, 128
GB = 4
STREAMS = 4
ROUNDS = BATCH // (GB * STREAMS)
GW = GB * D
SKIPS = 4
LN_EPS = 1e-5
GATE_I, GATE_F, GATE_G, GATE_O = range(4)
HALF = GW // 2
CELLS = [(1, 0, 0, GB // 2), (1, 0, GB // 2, GB // 2)] + [(p, j, 0, GB) for p in range(2, SKIPS + 1) for j in range(p)]


class Tally:

    def __init__(self, sem, base=0):
        self.sem, self.base, self.n = sem, base, 0

    def did(self, ins):
        ins.then_inc(self.sem, 1)
        self.n += 1

    def last(self, eng):
        eng.wait_ge(self.sem, self.base + self.n)


def build(nc, t_in, out):
    with ExitStack() as ctx:
        def sb(name, shape, dt=F32):
            return ctx.enter_context(nc.sbuf_tensor(name, shape, dt))

        def sem(name):
            return ctx.enter_context(nc.semaphore(name))

        banks = [ctx.enter_context(nc.psum_tensor(f"bank{i}", [128, 512], F32)) for i in range(8)]
        adj = sb("adj", [N, N])
        ident = sb("ident", [N, N + 1])
        ones = sb("ones", [N, N])
        below = sb("below", [N, N + 1])
        iota_f = sb("iota_f", [N, N])
        iota_p = sb("iota_p", [N, 1])
        grid = sb("grid", [N, F])
        Lap = sb("Lap", [N, N])
        A = sb("A", [N, N])
        uB = sb("uB", [N, N])
        u_c = sb("u_c", [N, 1])
        wB = sb("wB", [N, N])
        sc = sb("sc", [N, 64])
        scp = sb("scp", [N, 64])
        Um = sb("Um", [N, N])
        hB = sb("hB", [N, N])
        eB = sb("eB", [N, N])
        dB = sb("dB", [N, N])
        m = [sb(f"m{i}", [N, N]) for i in range(10)]
        PV = sb("PV", [N, N * F])
        RC = sb("RC", [N, N * LANES])
        NE = sb("NE", [N, N * LANES])
        BIG = sb("BIG", [N, N * F])
        leaf = sb("leaf", [N, 8 * LEAF + 64])
        leaf3 = sb("leaf3", [N, 10 * LEAF])
        leaf2 = sb("leaf2", [N, 7 * LEAF])
        U = sb("U", [N, N])
        UT = sb("UT", [N, N])
        QT = sb("QT", [N, N])
        cnt = sb("cnt", [N, F])
        XG = sb("XG", [N, F])
        r32 = sb("r32", [N, F])
        D4 = sb("D4", [N, LEVELS, N])
        EV = sb("EV", [N, LEVELS, N])
        E4 = sb("E4", [N, LEVELS, N])
        wrow = sb("wrow", [N, 6, N])
        V4 = sb("V4", [N, LEVELS, N])
        lam4 = sb("lam4", [N, LEVELS])

        X = sb("X", [N, BATCH, D])
        stats = sb("stats", [N, BATCH, 6])
        ln = sb("ln", [N, 4, BATCH])
        wT = sb("wT", [N, 2, SKIPS, 4 * D])
        adjT = sb("adjT", [N, N])
        bias_nat = sb("bias_nat", [4 * SKIPS, 2, D])
        bias = sb("bias", [N, 4 * SKIPS])
        W1, W2, Wg0, Wg1 = sb("W1", [N, D]), sb("W2", [N, D]), sb("Wg0", [N, D]), sb("Wg1", [N, D])
        b1 = sb("b1", [N, 1])
        b2B, bg0B, bg1B = sb("b2B", [N, D]), sb("bg0B", [N, D]), sb("bg1B", [N, D])
        G0 = sb("G0", [N, N])
        spare = sb("spare", [N, 16 * GW])
        w_nat = spare[:, 0:2 * SKIPS * 4 * D].rearrange("n (c p g h) -> n c p g h", c=2, p=SKIPS, g=4)

        x_in = sem("x_in")
        weights_in = sem("weights_in")
        small_in = sem("small_in")
        w_turned = sem("w_turned")
        w_kept = sem("w_kept")
        small_turned = sem("small_turned")
        ln_var = sem("ln_var")
        ln_dev = sem("ln_dev")
        ln_done = sem("ln_done")
        eig_done = sem("eig_done")

        def per_stream(name):
            return [sem(f"{name}{i}") for i in range(STREAMS)]

        h_ready, agg_ready, agg_kept, hid_ready, relu_ready = map(per_stream, ("h", "agg", "aggk", "hid", "relu"))
        out_ready, out_kept, back_ready, x1_ready = map(per_stream, ("o", "ok", "back", "x1"))
        h1_ready, mix_ready, mix_kept, lin_ready, lin_kept = map(per_stream, ("h1", "mix", "mixk", "lin", "link"))
        y_ready, z_ready, z_kept, conv_ready, H_ready = map(per_stream, ("y", "z", "zk", "conv", "H"))
        gates_ready, acts_ready, cell_part, cell_ready = map(per_stream, ("gates", "acts", "cellp", "cell"))
        tanh_ready, hidden_ready, turned_ready, sum_ready = map(per_stream, ("tanh", "hidden", "turned", "sum"))

        bn_done = sem("bn_done")
        PARTS = sum(2 for _, j, _, _ in CELLS if j)
        adj_in = sem("adj_in")
        consts = sem("consts")
        v_ = sem("v_")
        hv = sem("hv")
        x_ready = sem("x_ready")
        xb_ready = sem("xb_ready")
        s2_ready = sem("s2_ready")
        sigma_ready = sem("sigma_ready")
        u_ready = sem("u_ready")
        um_kept = sem("um_kept")
        p_ready = sem("p_ready")
        a_ready = sem("a_ready")
        leaf_ready = sem("leaf_ready")
        leaf_sign = sem("leaf_sign")
        to_pe = sem("to_pe")
        from_pe = sem("from_pe")
        rs_in = sem("rs_in")
        rs_out = sem("rs_out")
        st1, st2, tw1, tw2 = sem("st1"), sem("st2"), sem("tw1"), sem("tw2")
        pool_s = sem("pool_s")
        pool_q = sem("pool_q")
        stv = sem("stv")
        stored = sem("stored")
        block = ctx.enter_context(nc.Block())

        STEPS = N - 1

        d16, e16 = leaf[:, 0:16], leaf[:, 16:32]
        am = leaf[:, 32:48]
        tmp = leaf[:, 48:64]
        oh = leaf[:, 64:80]
        runs = [leaf2[:, 0:32], leaf2[:, 32:64]]
        pick = leaf2[:, 64:112].rearrange("p (c f) -> p c f", f=LEAF)
        sg = leaf[:, 96:160]
        pi, rho, w16, we, y16, ey, c16, gam, ne16, neg16 = (leaf3[:, c * LEAF:(c + 1) * LEAF] for c in range(10))

        pieces = [BIG[:, c * GW:(c + 1) * GW] for c in range(8)] + [PV[:, c * GW:(c + 1) * GW] for c in range(8)] \
            + [spare[:, c * GW:(c + 1) * GW] for c in range(16)]
        gI, gF, gG, gO, cS, HS, tS, hS = ([pieces[STREAMS * c + i] for i in range(STREAMS)] for c in range(8))
        hs, mixS, linS, yS, zS = gI, gF, gG, gO, cS

        def batches(v):
            return v.rearrange("p (b t) -> p b t", b=GB)

        bank = [[banks[2 * i + c % 2][:] for c in range(4)] for i in range(STREAMS)]

        def gate(i, q, T):
            return banks[2 * i + (q in (GATE_F, GATE_O))][:, HALF * (q in (GATE_G, GATE_O)):][:, 0:T]
        x_dram = t_in["x"].rearrange("b n d -> n b d")
        out_dram = out.rearrange("b n d -> n b d")
        X_CHUNKS = 4

        @block.sync
        def _(sp):
            sp.dma_start(adj[:], t_in["adj"]).then_inc(adj_in, 16)
            for c in range(X_CHUNKS):
                r = slice(c * BATCH // X_CHUNKS, (c + 1) * BATCH // X_CHUNKS)
                sp.dma_start(X[:, r, :], x_dram[:, r, :]).then_inc(x_in, 16)
            for c, name in enumerate(("L1_gnn_Wih", "L1_gnn_Whh")):
                for p in range(SKIPS):
                    sp.dma_start(w_nat[:, c, p], t_in[name][p].rearrange("(g u) h -> u g h", g=4)).then_inc(weights_in, 16)
            for t, name in ((W1, "L0_gnn_W1"), (W2, "L0_gnn_W2"), (Wg0, "L1_gnn_Wg0"), (Wg1, "L1_gnn_Wg1")):
                sp.dma_start(t[:], t_in[name]).then_inc(small_in, 16)
            for t, name in ((b2B, "L0_gnn_b2"), (bg0B, "L1_gnn_bg0"), (bg1B, "L1_gnn_bg1")):
                sp.dma_start(t[:], t_in[name].rearrange("(a d) -> a d", a=1).to_broadcast([N, D])).then_inc(small_in, 16)
            sp.dma_start(b1[:], t_in["L0_gnn_b1"].rearrange("(d a) -> d a", a=1)).then_inc(small_in, 16)
            for c, name in enumerate(("L1_gnn_bih", "L1_gnn_bhh")):
                sp.dma_start(bias_nat[:, c, :], t_in[name].rearrange("p (g u) -> (p g) u", g=4)).then_inc(small_in, 16)
            with nc.sync.Fori(0, ROUNDS) as it:
                for i in range(STREAMS):
                    b = bass.ds(it * (STREAMS * GB) + i * GB, GB)
                    sp.wait_ge(sum_ready[i], it + 2)
                    sp.dma_start(out_dram[:, b, :], X[:, b, :]).then_inc(stored, 16)
            sp.wait_ge(stored, 16 * ROUNDS * STREAMS)

        @block.gpsimd
        def _(pool):
            p = Tally(consts)
            nc.gpsimd.memset(ones[:], 1.0).then_inc(pool_s, 1)
            pool.wait_ge(pool_s, 1)
            p.did(nc.gpsimd.affine_select(out=ident[:, 0:N], in_=ones[:], compare_op=ALU.is_equal, fill=0.0,
                                          base=0, pattern=[[-1, N]], channel_multiplier=1))
            p.did(nc.gpsimd.affine_select(out=below[:, 0:N], in_=ones[:], compare_op=ALU.is_gt, fill=0.0,
                                          base=0, pattern=[[-1, N]], channel_multiplier=1))
            p.did(nc.gpsimd.iota(iota_f[:], pattern=[[1, N]], base=0, channel_multiplier=0,
                                 allow_small_or_imprecise_dtypes=True))
            p.did(nc.gpsimd.iota(iota_p[:], pattern=[[1, 1]], base=0, channel_multiplier=1,
                                 allow_small_or_imprecise_dtypes=True))
            p.did(nc.gpsimd.iota(grid[:], pattern=[[1, F]], base=0, channel_multiplier=F,
                                 allow_small_or_imprecise_dtypes=True))
            p.did(nc.gpsimd.memset(leaf2[:], 1.0))
            p.did(nc.gpsimd.memset(sg, 1.0))
            pool.wait_ge(consts, 7)

            pool.wait_ge(leaf_ready, 1)
            S = lambda i, n=1: sg[:, i:i + n]
            PAR, NEG1, HALF, T0, R_, P_, SIG, OG = 0, 2, 4, 10, 12, 14, 16, 18
            q = Tally(pool_q)

            def op(ins):
                q.did(ins)
                q.last(pool)

            op(nc.gpsimd.memset(S(NEG1, 2), -1.0))
            op(nc.gpsimd.memset(S(HALF, 2), 0.5))
            op(nc.gpsimd.memset(leaf3[:], 1.0))
            op(nc.gpsimd.memset(neg16, -1.0))
            TT = nc.gpsimd.tensor_tensor
            TS = nc.gpsimd.tensor_scalar
            with nc.gpsimd.Fori(0, QR_SWEEPS) as k:
                pool.sem_clear(pool_q)
                q = Tally(pool_q)

                def op(ins):
                    q.did(ins)
                    q.last(pool)
                op(TT(tmp[:, 0:15], d16[:, 0:15], d16[:, 1:16], ALU.mult))
                op(TS(tmp[:, 0:15], tmp[:, 0:15], QR_EPS2, None, ALU.mult))
                op(TT(tmp[:, 0:15], e16[:, 0:15], tmp[:, 0:15], ALU.subtract))
                op(TS(tmp[:, 0:15], tmp[:, 0:15], 0.0, None, ALU.is_gt))
                op(TT(e16[:, 0:15], e16[:, 0:15], tmp[:, 0:15], ALU.mult))
                op(TS(runs[0][:, 0:14], tmp[:, 1:15], -1.0, 1.0, ALU.mult, ALU.add))
                for c in range(4):
                    op(TT(runs[(c + 1) % 2][:, 0:LEAF], runs[c % 2][:, 0:LEAF],
                          runs[c % 2][:, 2 ** c:LEAF + 2 ** c], ALU.mult))
                op(TT(oh[:, 0:15], runs[0][:, 0:15], tmp[:, 0:15], ALU.mult))
                for c, v in enumerate((d16[:, 1:16], d16[:, 0:15], e16[:, 0:15])):
                    op(TT(pick[:, c, 0:15], v, oh[:, 0:15], ALU.mult))
                op(nc.gpsimd.memset(pick[:, :, 15:16], 0.0))
                for w in (8, 4, 2, 1):
                    op(TT(pick[:, :, 0:w], pick[:, :, 0:w], pick[:, :, w:2 * w], ALU.add))
                op(nc.gpsimd.tensor_copy(S(SIG), pick[:, 0, 0:1]))
                op(nc.gpsimd.tensor_copy(S(T0), pick[:, 1, 0:1]))
                op(nc.gpsimd.tensor_copy(S(R_), pick[:, 2, 0:1]))
                op(TS(S(T0), S(T0), S(SIG), 0.5, ALU.subtract, ALU.mult))
                op(TT(S(P_), S(T0), S(T0), ALU.mult))
                op(TS(S(P_), S(P_), S(R_), TINY, ALU.add, ALU.add))
                op(TT(S(P_), S(P_), S(HALF), ALU.pow))
                op(TS(S(OG), S(T0), 0.0, 2.0, ALU.is_ge, ALU.mult))
                op(TS(S(OG), S(OG), 1.0, S(P_), ALU.subtract, ALU.mult))
                op(TT(S(OG), S(OG), S(T0), ALU.add))
                op(TT(S(OG), S(OG), S(NEG1), ALU.pow))
                op(TT(S(OG), S(OG), S(R_), ALU.mult))
                op(TT(S(SIG), S(SIG), S(OG), ALU.subtract))
                op(TS(am, d16, S(SIG), 1e-15, ALU.subtract, ALU.add))
                op(TS(S(T0), am[:, 0:1], 0.0, -2.0, ALU.is_ge, ALU.mult))
                op(TS(S(PAR), S(T0), 1.0, S(PAR), ALU.add, ALU.mult))
                op(TS(ne16, e16, -1.0, None, ALU.mult))
                op(nc.gpsimd.tensor_copy(pi[:, 0:1], am[:, 0:1]))
                op(TT(rho[:, 0:1], pi[:, 0:1], neg16[:, 0:1], ALU.pow))
                for i in range(LEAF - 1):
                    op(TS(pi[:, i + 1:i + 2], rho[:, i:i + 1], ne16[:, i:i + 1], am[:, i + 1:i + 2],
                          ALU.mult, ALU.add))
                    op(TT(rho[:, i + 1:i + 2], pi[:, i + 1:i + 2], neg16[:, 0:1], ALU.pow))
                op(TT(w16, rho, rho, ALU.mult))
                op(TT(we[:, 1:LEAF], w16[:, 1:LEAF], e16[:, 0:LEAF - 1], ALU.mult))
                op(nc.gpsimd.tensor_copy(y16[:, 0:1], w16[:, 0:1]))
                for i in range(1, LEAF):
                    op(TS(y16[:, i:i + 1], y16[:, i - 1:i], we[:, i:i + 1], w16[:, i:i + 1], ALU.mult, ALU.add))
                op(TT(ey[:, 0:LEAF], e16, y16, ALU.mult))
                op(TS(c16[:, 1:LEAF], ey[:, 0:LEAF - 1], 1.0, None, ALU.add))
                op(TT(c16[:, 1:LEAF], c16[:, 1:LEAF], neg16[:, 1:LEAF], ALU.pow))
                op(TT(ey[:, 0:LEAF - 1], ey[:, 0:LEAF - 1], c16[:, 1:LEAF], ALU.mult))
                op(TT(gam, c16, pi, ALU.mult))
                op(TT(y16, y16, neg16, ALU.pow))
                op(TT(y16, y16, e16, ALU.add))
                op(TT(e16[:, 0:LEAF - 1], ey[:, 0:LEAF - 1], y16[:, 1:LEAF], ALU.mult))
                op(TT(d16[:, 0:LEAF - 1], d16[:, 1:LEAF], gam[:, 0:LEAF - 1], ALU.add))
                op(TT(d16[:, 0:LEAF - 1], d16[:, 0:LEAF - 1], gam[:, 1:LEAF], ALU.subtract))
                op(TT(d16[:, LEAF - 1:LEAF], S(SIG), gam[:, LEAF - 1:LEAF], ALU.add))
                assert q.n == QR_PER, q.n
            nc.gpsimd.tensor_copy(S(PAR), S(PAR)).then_inc(leaf_sign, 1)

        @block.scalar
        def _(act):
            act.wait_ge(rs_in, 1)
            nc.scalar.activation(m[5][:], m[4][:], ACT.Sqrt).then_inc(rs_out, 1)
            for k in range(STEPS):
                act.wait_ge(s2_ready, k + 1)
                nc.scalar.activation(sc[:, 0:1], banks[5][:, 0:1], ACT.Sqrt).then_inc(sigma_ready, 1)
                act.wait_ge(u_ready, k + 1)
                nc.scalar.activation(Um[:, k:k + 1], u_c[:], ACT.Copy).then_inc(um_kept, 1)
            for c in range(2 * SKIPS):
                act.wait_ge(w_turned, c + 1)
                nc.scalar.activation(wT[:, c // SKIPS, c % SKIPS, :], banks[c % 2][:], ACT.Copy).then_inc(w_kept, 1)
            act.wait_ge(small_turned, 1)
            nc.scalar.activation(adjT[:], banks[0][:, 0:N], ACT.Copy).then_inc(w_kept, 1)
            nc.scalar.activation(bias[:], banks[0][:, N:N + 4 * SKIPS], ACT.Copy).then_inc(w_kept, 1)
            act.wait_ge(small_turned, 2)
            nc.scalar.activation(G0[:], banks[1][:, 0:N], ACT.Copy).then_inc(w_kept, 1)
            act.wait_ge(ln_var, 1)
            nc.scalar.activation(ln[:, 2, :], ln[:, 1, :], ACT.Sqrt).then_inc(ln_dev, 1)
            act.wait_ge(rs_in, 2)
            nc.scalar.activation(sc[:, 24:28], sc[:, 20:24], ACT.Sqrt).then_inc(rs_out, 1)

            def batch(it, i, b):
                return it * (STREAMS * GB) + (i * GB + b)

            def normalize(it, i, done):
                for b in range(GB):
                    at = bass.ds(batch(it, i, b), 1)
                    last = nc.scalar.activation(hs[i][:, b * D:(b + 1) * D],
                                                X[:, at, :].rearrange("p b d -> p (b d)"), ACT.Relu,
                                                bias=ln[:, 3, at], scale=ln[:, 2, at])
                last.then_inc(done, 1)

            act.wait_ge(eig_done, 1)
            act.wait_ge(ln_done, 1)
            with nc.scalar.Fori(0, ROUNDS) as it:
                for i in range(STREAMS):
                    normalize(it, i, h_ready[i])
                for i in range(STREAMS):
                    act.wait_ge(hid_ready[i], it + 1)
                    nc.scalar.activation(linS[i], bank[i][1], ACT.Relu, bias=b1[:, 0:1]).then_inc(relu_ready[i], 1)
            act.wait_ge(ln_var, 2)
            nc.scalar.activation(ln[:, 2, :], ln[:, 1, :], ACT.Sqrt).then_inc(ln_dev, 1)
            act.wait_ge(ln_done, 2)
            with nc.scalar.Fori(0, ROUNDS) as it:
                for i in range(STREAMS):
                    normalize(it, i, h1_ready[i])
                for i in range(STREAMS):
                    act.wait_ge(lin_kept[i], it + 1)
                    nc.scalar.activation(yS[i], linS[i], ACT.Relu).then_inc(y_ready[i], 1)
                for i in range(STREAMS):
                    act.wait_ge(conv_ready[i], it + 1)
                    nc.scalar.activation(HS[i], bank[i][3], ACT.Relu).then_inc(H_ready[i], 1)
                for c, (p, j, _, nb) in enumerate(CELLS):
                    T = nb * (N // p)
                    for i in range(STREAMS):
                        act.wait_ge(gates_ready[i], it * len(CELLS) + c + 1)
                        for q, g, f in ((GATE_I, gI, ACT.Sigmoid), (GATE_G, gG, ACT.Tanh), (GATE_F, gF, ACT.Sigmoid),
                                        (GATE_O, gO, ACT.Sigmoid)):
                            if q == GATE_F and j == 0:
                                continue
                            at = (p - 1) * 4 + q
                            last = nc.scalar.activation(g[i][:, 0:T], gate(i, q, T), f, bias=bias[:, at:at + 1])
                        last.then_inc(acts_ready[i], 1)
                    for i in range(STREAMS):
                        act.wait_ge(cell_ready[i], it * len(CELLS) + c + 1)
                        nc.scalar.activation(tS[i][:, 0:T], cS[i][:, 0:T], ACT.Tanh).then_inc(tanh_ready[i], 1)

        B = [b[:, 0:N] for b in banks]
        M = [x[:] for x in m]

        @block.tensor
        def _(pe):
            n = [0]

            def mms(*jobs):
                n[0] += 1
                pe.wait_ge(to_pe, n[0])
                for j in jobs:
                    if len(j) == 2:
                        last = nc.tensor.transpose(j[0], j[1], ident[:, 0:N])
                    else:
                        last = nc.tensor.matmul(j[0], j[1], j[2], start=True, stop=True)
                last.then_inc(from_pe, 1)

            def householder(k):
                pe.wait_ge(x_ready, k + 1)
                nc.tensor.matmul(banks[5][:, 0:1], ident[:, N:N + 1].to_broadcast([N, N]), ident[:, N:N + 1],
                                 start=True, stop=True).then_inc(s2_ready, 1)
                nc.tensor.matmul(B[0], ident[:, N:N + 1].to_broadcast([N, N]), ident[:, 0:N],
                                 start=True, stop=True).then_inc(xb_ready, 1)
                pe.wait_ge(u_ready, k + 1)
                pe.wait_ge(a_ready, k + 1)
                nc.tensor.matmul(banks[2][:, 0:1], A[:], u_c[:], start=True, stop=True)
                nc.tensor.matmul(B[1], u_c[:].to_broadcast([N, N]), A[:],
                                 start=True, stop=True).then_inc(p_ready, 1)

            mms((B[3], ones[:], M[0]))
            mms((B[3], M[6]))
            for k in range(LEAF):
                householder(k)
            mms((B[3], ones[:], M[2]))
            for k in range(LEAF, STEPS):
                householder(k)
            mms((B[3], ones[:], M[2]), (B[4], Um[:], Um[:]))
            mms((B[3], M[1]), (B[4], Um[:]))
            mms((B[3], M[1], M[0]), (B[4], M[0], M[1]))
            for r in range(6):
                if r < 5:
                    mms((B[5], M[4], M[6]), (B[3], M[4], M[3]), (B[4], M[3], M[4]))
                else:
                    mms((B[5], M[4], M[6]))
            mms((B[3], M[7], M[8]))
            mms((B[3], M[8], M[5]))
            pe.wait_ge(weights_in, 16 * 2 * SKIPS)
            for c in range(2 * SKIPS):
                if c >= 2:
                    pe.wait_ge(w_kept, c - 1)
                for q in range(4):
                    last = nc.tensor.transpose(banks[c % 2][:, q * D:(q + 1) * D], w_nat[:, c // SKIPS, c % SKIPS, q, :],
                                               ident[:, 0:N])
                last.then_inc(w_turned, 1)
            pe.wait_ge(small_in, 16 * 10)
            pe.wait_ge(w_kept, 2 * SKIPS)
            nc.tensor.transpose(banks[0][:, 0:N], adj[:], ident[:, 0:N])
            K = 4 * SKIPS
            nc.tensor.matmul(banks[0][:, N:N + K], bias_nat[:, 0, :], ident[0:K, 0:K], start=True, stop=False)
            nc.tensor.matmul(banks[0][:, N:N + K], bias_nat[:, 1, :], ident[0:K, 0:K],
                             start=False, stop=True).then_inc(small_turned, 1)
            pe.wait_ge(w_kept, 2 * SKIPS + 2)
            nc.tensor.matmul(banks[1][:, 0:N], bg0B[:], adjT[:], start=True, stop=True).then_inc(small_turned, 1)
            for f in range(F):
                pe.wait_ge(stv, f + 1)
                ins = nc.tensor.matmul(banks[6][:, 0:1], BIG[:, f * N:(f + 1) * N], ones[:, 0:1],
                                       start=(f == 0), stop=(f == F - 1))
            ins.then_inc(from_pe, 1)
            mms((B[3], V4[:, 0, :]), (banks[6][:, 0:1], sc[:, 30:31].to_broadcast([N, N]), ones[:, 0:1]))
            mms((B[3], M[1], QT[:]), (B[4], QT[:], M[1]), (banks[5][:, 0:1], QT[:], sc[:, 31:32]))
            for r in range(REFINES):
                mms((B[3], Lap[:], U[:]))
                mms((B[4], U[:], M[0]), (B[5], U[:], U[:]))
                mms((B[6], ones[:], M[5]))
                mms((B[3], UT[:], M[5]), (B[4], M[5], UT[:]))
            mms((banks[3][:, 0:1], U[:], sc[:, 32:33]))
            mms((B[4], UT[:]))

            pe.wait_ge(eig_done, 1)
            with nc.tensor.Fori(0, ROUNDS) as it:
                for i in range(STREAMS):
                    pe.wait_ge(h_ready[i], it + 1)
                    for b in range(GB):
                        last = nc.tensor.matmul(bank[i][0][:, b * N:(b + 1) * N], hs[i][:, b * D:(b + 1) * D], U[:],
                                                start=True, stop=True)
                    last.then_inc(agg_ready[i], 1)
                for i in range(STREAMS):
                    pe.wait_ge(agg_kept[i], it + 1)
                    nc.tensor.matmul(bank[i][1], W1[:], mixS[i], start=True, stop=True).then_inc(hid_ready[i], 1)
                for i in range(STREAMS):
                    pe.wait_ge(relu_ready[i], it + 1)
                    for b in range(GB):
                        last = nc.tensor.matmul(bank[i][2][:, b * D:(b + 1) * D], linS[i][:, b * N:(b + 1) * N], W2[:],
                                                start=True, stop=True)
                    last.then_inc(out_ready[i], 1)
                for i in range(STREAMS):
                    pe.wait_ge(out_kept[i], it + 1)
                    nc.tensor.matmul(bank[i][3], UT[:], zS[i], start=True, stop=True).then_inc(back_ready[i], 1)
            with nc.tensor.Fori(0, ROUNDS) as it:
                for i in range(STREAMS):
                    pe.wait_ge(h1_ready[i], it + 1)
                    pe.wait_ge(sum_ready[i], it + 1)
                    for b in range(GB):
                        last = nc.tensor.matmul(bank[i][0][:, b * N:(b + 1) * N], hs[i][:, b * D:(b + 1) * D], adjT[:],
                                                start=True, stop=True)
                    last.then_inc(mix_ready[i], 1)
                for i in range(STREAMS):
                    pe.wait_ge(mix_kept[i], it + 1)
                    nc.tensor.matmul(bank[i][1], Wg0[:], mixS[i], start=True, stop=True).then_inc(lin_ready[i], 1)
                for i in range(STREAMS):
                    pe.wait_ge(y_ready[i], it + 1)
                    for b in range(GB):
                        last = nc.tensor.matmul(bank[i][2][:, b * D:(b + 1) * D], yS[i][:, b * N:(b + 1) * N], Wg1[:],
                                                start=True, stop=True)
                    last.then_inc(z_ready[i], 1)
                for i in range(STREAMS):
                    pe.wait_ge(z_kept[i], it + 1)
                    for b in range(GB):
                        last = nc.tensor.matmul(bank[i][3][:, b * N:(b + 1) * N], zS[i][:, b * D:(b + 1) * D], adjT[:],
                                                start=True, stop=True)
                    last.then_inc(conv_ready[i], 1)
                for c, (p, j, b0, nb) in enumerate(CELLS):
                    W = N // p
                    for i in range(STREAMS):
                        if c == 0:
                            pe.wait_ge(H_ready[i], it + 1)
                        else:
                            pe.wait_ge(hidden_ready[i], it * len(CELLS) + c)
                        xt = batches(HS[i])[:, b0:b0 + nb, j:(W - 1) * p + j + 1:p]
                        for q in (GATE_I, GATE_G, GATE_F, GATE_O):
                            if q == GATE_F and j == 0:
                                continue
                            dst = gate(i, q, nb * W)
                            r = slice(q * D, (q + 1) * D)
                            last = nc.tensor.matmul(dst, wT[:, 0, p - 1, r], xt, start=True, stop=(j == 0))
                            if j:
                                last = nc.tensor.matmul(dst, wT[:, 1, p - 1, r], hS[i][:, 0:GB * W],
                                                        start=False, stop=True)
                        last.then_inc(gates_ready[i], 1)
                for i in range(STREAMS):
                    pe.wait_ge(hidden_ready[i], it * len(CELLS) + len(CELLS))
                    for b in range(GB):
                        last = nc.tensor.transpose(bank[i][0][:, b * D:(b + 1) * D], HS[i][:, b * N:(b + 1) * N],
                                                   ident[:, 0:N])
                    last.then_inc(turned_ready[i], 1)

        @block.vector
        def _(dve):
            t = Tally(v_)
            V = nc.vector
            asked, answered = [0], [0]

            def op(ins):
                t.did(ins)
                t.last(dve)

            def ask(ins):
                ins.then_inc(to_pe, 1)
                asked[0] += 1
                answered[0] += 1
                dve.wait_ge(from_pe, answered[0])

            def S(i, n=1):
                return sc[:, i:i + n]

            def total(dst, a, b, alu=ALU.add, junk=None):
                op(V.tensor_tensor_reduce(out=(m[9][:] if junk is None else junk), in0=a, in1=b, scale=1.0, scalar=0.0,
                                          op0=ALU.mult, op1=alu, accum_out=dst))

            I = ident[:, 0:N]
            op(V.memset(sc[:], 0.0))
            op(V.memset(eB[:], 0.0))
            op(V.memset(hB[:], 0.0))
            op(V.memset(Um[:], 0.0))
            dve.wait_ge(adj_in, 16)
            dve.wait_ge(consts, 7)
            op(V.tensor_reduce(S(1), adj[:], AX_X, ALU.add))
            total(S(2), adj[:], I)
            op(V.tensor_tensor(S(3), S(1), S(2), ALU.subtract))
            ask(V.scalar_tensor_tensor(out=M[0], in0=I, scalar=S(3), in1=adj[:], op0=ALU.mult, op1=ALU.add))
            op(V.tensor_copy(M[1], B[3]))
            op(V.tensor_scalar(M[3], M[1], 0.0, None, ALU.is_gt))
            V.tensor_scalar(M[4], M[1], TINY, None, ALU.max).then_inc(rs_in, 1)
            dve.wait_ge(rs_in, 1)
            dve.wait_ge(rs_out, 1)
            op(V.reciprocal(M[5], M[5]))
            op(V.tensor_tensor(M[2], M[5], M[5], ALU.mult))
            op(V.tensor_tensor(M[2], M[2], M[4], ALU.mult))
            op(V.tensor_scalar(M[2], M[2], -0.5, 1.5, ALU.mult, ALU.add))
            op(V.tensor_tensor(M[2], M[2], M[5], ALU.mult))
            op(V.tensor_tensor(M[4], M[2], M[3], ALU.mult))
            total(S(7), M[4], I)
            op(V.tensor_tensor(M[5], M[1], I, ALU.mult))
            op(V.tensor_tensor(M[5], M[5], adj[:], ALU.subtract))
            ask(V.scalar_tensor_tensor(out=M[6], in0=M[5], scalar=S(7), in1=M[4], op0=ALU.mult, op1=ALU.mult))
            op(V.tensor_tensor(Lap[:], M[6], B[3], ALU.add))
            op(V.tensor_scalar(Lap[:], Lap[:], 0.5, None, ALU.mult))
            op(V.tensor_tensor(ident[:, N:N + 1], Lap[:, 0:1], below[:, 0:1], ALU.mult))
            V.tensor_copy(A[:], Lap[:]).then_inc(a_ready, 1)
            V.tensor_copy(sc[:, 40:41], sc[:, 1:2]).then_inc(x_ready, 1)

            HV = 14
            SS, DEN, G_, K2, NHU, NHW, WC, TX = 10, 11, 12, 13, 14, 15, 16, 17

            def householder(k, base):
                h = Tally(hv, base)

                def op(ins):
                    h.did(ins)
                    h.last(dve)

                nxt = slice(k + 1, k + 2)
                dve.wait_ge(xb_ready, k + 1)
                dve.wait_ge(a_ready, k + 1)
                op(V.tensor_copy(uB[:], B[0]))
                op(V.tensor_scalar(S(SS), uB[:, nxt], 0.0, 2.0, ALU.is_ge, ALU.mult))
                dve.wait_ge(sigma_ready, k + 1)
                op(V.tensor_scalar(S(SS), S(SS), 1.0, S(0), ALU.subtract, ALU.mult))
                if k:
                    dve.wait_ge(um_kept, k)
                V.scalar_tensor_tensor(out=u_c[:], in0=ident[:, nxt], scalar=S(SS), in1=ident[:, N:N + 1],
                                       op0=ALU.mult, op1=ALU.add).then_inc(u_ready, 1)
                op(V.scalar_tensor_tensor(out=S(DEN), in0=uB[:, nxt], scalar=S(SS), in1=banks[5][:, 0:1],
                                          op0=ALU.mult, op1=ALU.add))
                op(V.tensor_scalar(S(DEN), S(DEN), TINY, None, ALU.add))
                op(V.reciprocal(hB[:, k:k + 1], S(DEN)))
                op(V.tensor_copy(eB[:, k:k + 1], S(SS)))
                op(V.tensor_tensor(uB[:, nxt], uB[:, nxt], S(SS), ALU.add))
                dve.wait_ge(u_ready, k + 1)
                hk = hB[:, k:k + 1]
                op(V.tensor_scalar(S(NHU), u_c[:], hk, -1.0, ALU.mult, ALU.mult))
                dve.wait_ge(p_ready, k + 1)
                op(V.tensor_tensor_reduce(out=wB[:], in0=B[1], in1=uB[:], scale=1.0, scalar=0.0,
                                          op0=ALU.mult, op1=ALU.add, accum_out=S(G_)))
                op(V.tensor_scalar(S(K2), S(G_), hk, -0.5, ALU.mult, ALU.mult))
                op(V.scalar_tensor_tensor(out=S(WC), in0=u_c[:], scalar=S(K2), in1=banks[2][:, 0:1],
                                          op0=ALU.mult, op1=ALU.add))
                op(V.scalar_tensor_tensor(out=wB[:], in0=uB[:], scalar=S(K2), in1=B[1],
                                          op0=ALU.mult, op1=ALU.add))
                op(V.tensor_scalar(S(NHW), S(WC), hk, -1.0, ALU.mult, ALU.mult))
                op(V.scalar_tensor_tensor(out=S(TX), in0=wB[:, nxt], scalar=S(NHU), in1=A[:, nxt],
                                          op0=ALU.mult, op1=ALU.add))
                op(V.scalar_tensor_tensor(out=S(TX), in0=uB[:, nxt], scalar=S(NHW), in1=S(TX),
                                          op0=ALU.mult, op1=ALU.add))
                V.tensor_tensor(ident[:, N:N + 1], S(TX), below[:, nxt], ALU.mult).then_inc(x_ready, 1)
                op(V.scalar_tensor_tensor(out=A[:], in0=wB[:], scalar=S(NHU), in1=A[:], op0=ALU.mult, op1=ALU.add))
                V.scalar_tensor_tensor(out=A[:], in0=uB[:], scalar=S(NHW), in1=A[:],
                                       op0=ALU.mult, op1=ALU.add).then_inc(a_ready, 1)
                return h.n

            HPER = 17
            n1 = householder(0, 0)
            assert n1 == HPER, n1
            for k in range(1, LEAF):
                householder(k, k * HPER)
            dve.wait_ge(a_ready, LEAF + 1)
            dve.wait_ge(x_ready, LEAF + 1)
            ask(V.tensor_tensor(M[2], A[:], I, ALU.mult))
            op(V.tensor_copy(d16, banks[3][:, 0:LEAF]))
            op(V.tensor_tensor(e16, eB[:, 0:LEAF], eB[:, 0:LEAF], ALU.mult))
            op(V.memset(e16[:, LEAF - 1:LEAF], 0.0))
            op(V.scalar_tensor_tensor(out=S(8), in0=eB[:, LEAF - 1:LEAF], scalar=-1.0, in1=eB[:, LEAF - 1:LEAF],
                                      op0=ALU.mult, op1=ALU.max))
            V.tensor_tensor(d16[:, LEAF - 1:LEAF], d16[:, LEAF - 1:LEAF], S(8), ALU.subtract).then_inc(leaf_ready, 1)
            for k in range(LEAF, STEPS):
                householder(k, k * HPER)
            dve.wait_ge(a_ready, N)
            dve.wait_ge(um_kept, STEPS)

            dve.wait_ge(x_in, 16 * X_CHUNKS)
            for b in range(BATCH):
                V.bn_stats(stats[:, b, :], X[:, b, :]).then_inc(bn_done, 1)
            dve.wait_ge(bn_done, BATCH)

            def deviations(n):
                st = stats[:].rearrange("p b s -> p s b")
                mean, var, inv, off = (ln[:, c, :] for c in range(4))
                op(V.tensor_tensor(mean, st[:, 1, :], st[:, 4, :], ALU.subtract))
                op(V.tensor_tensor(off, mean, mean, ALU.mult))
                op(V.tensor_tensor(var, st[:, 2, :], st[:, 5, :], ALU.add))
                op(V.scalar_tensor_tensor(out=var, in0=off, scalar=D / 4.0, in1=var, op0=ALU.mult, op1=ALU.add))
                op(V.tensor_tensor(mean, st[:, 1, :], st[:, 4, :], ALU.add))
                V.tensor_scalar(var, var, 1.0 / D, LN_EPS, ALU.mult, ALU.add).then_inc(ln_var, 1)
                dve.wait_ge(ln_var, n)
                dve.wait_ge(ln_dev, n)
                op(V.reciprocal(inv, inv))
                op(V.tensor_tensor(off, inv, inv, ALU.mult))
                op(V.tensor_tensor(off, off, var, ALU.mult))
                op(V.tensor_scalar(off, off, -0.5, 1.5, ALU.mult, ALU.add))
                op(V.tensor_tensor(inv, off, inv, ALU.mult))
                V.scalar_tensor_tensor(out=off, in0=mean, scalar=-0.5, in1=inv, op0=ALU.mult, op1=ALU.mult)\
                    .then_inc(ln_done, 1)

            ask(V.tensor_tensor(M[2], A[:], I, ALU.mult))
            op(V.tensor_copy(dB[:], B[3]))
            op(V.tensor_tensor(M[1], B[4], below[:, 0:N], ALU.mult))
            ask(V.tensor_tensor(M[1], M[1], hB[:], ALU.mult))
            op(V.tensor_copy(M[0], B[3]))
            op(V.tensor_copy(M[8], B[4]))
            ask(V.tensor_tensor(M[6], I, M[0], ALU.subtract))
            for r in range(6):
                op(V.tensor_copy(M[3], B[3]))
                ask(V.tensor_copy(M[4], B[4]))
                op(V.tensor_tensor(M[6], M[6], B[5], ALU.add))
            ask(V.tensor_tensor(M[7], M[6], hB[:], ALU.mult))
            ask(V.tensor_copy(M[5], B[3]))
            op(V.tensor_tensor(QT[:], I, B[3], ALU.subtract))

            deviations(1)

            LO, HI, H1, H2, LAM = 18, 19, 33, 34, 35
            op(V.scalar_tensor_tensor(out=M[0], in0=eB[:], scalar=-1.0, in1=eB[:], op0=ALU.mult, op1=ALU.max))
            op(V.tensor_copy(M[1], M[0]))
            op(V.tensor_tensor(M[1][:, 1:N], M[1][:, 1:N], M[0][:, 0:N - 1], ALU.add))
            op(V.tensor_tensor(M[3], dB[:], M[1], ALU.subtract))
            op(V.tensor_reduce(S(LO), M[3], AX_X, ALU.min))
            op(V.tensor_tensor(M[3], dB[:], M[1], ALU.add))
            op(V.tensor_reduce(S(HI), M[3], AX_X, ALU.max))
            op(V.tensor_scalar(S(H1), S(HI), S(LO), 1.001 / (N * F), ALU.subtract, ALU.mult))
            op(V.scalar_tensor_tensor(out=S(LO), in0=S(H1), scalar=-0.5, in1=S(LO), op0=ALU.mult, op1=ALU.add))
            op(V.tensor_tensor(M[2], eB[:], eB[:], ALU.mult))
            op(V.tensor_scalar(M[2], M[2], TINY, -1.0, ALU.max, ALU.mult))
            PV3 = PV[:].rearrange("p (i f) -> p i f", f=F)

            def sturm(sem):
                op(V.tensor_tensor(PV3, dB[:].unsqueeze(2).to_broadcast([N, N, F]),
                                   XG[:].unsqueeze(1).to_broadcast([N, N, F]), ALU.subtract))
                s = Tally(sem)
                half = F // 2
                for i in range(N - 1):
                    for a in (0, half):
                        if i:
                            dve.wait_ge(sem, s.n - 1)
                        s.did(V.reciprocal(r32[:, a:a + half], PV[:, i * F + a:i * F + a + half]))
                    for a in (0, half):
                        dve.wait_ge(sem, s.n - 1)
                        nx = PV[:, (i + 1) * F + a:(i + 1) * F + a + half]
                        s.did(V.scalar_tensor_tensor(out=nx, in0=r32[:, a:a + half], scalar=M[2][:, i:i + 1],
                                                     in1=nx, op0=ALU.mult, op1=ALU.add))
                s.last(dve)
                op(V.tensor_scalar(PV[:], PV[:], 0.0, None, ALU.is_lt))
                op(V.tensor_reduce(cnt[:], PV[:].rearrange("p (i f) -> p f i", f=F), AX_X, ALU.add))

            op(V.tensor_scalar(XG[:], grid[:], S(H1), S(LO), ALU.mult, ALU.add))
            sturm(st1)
            for f in range(F):
                V.tensor_scalar(BIG[:, f * N:(f + 1) * N], iota_f[:], cnt[:, f:f + 1], None, ALU.is_ge).then_inc(stv, 1)
            answered[0] += 1
            dve.wait_ge(from_pe, answered[0])
            op(V.tensor_scalar(S(LAM), banks[6][:, 0:1], 1.0, S(H1), ALU.subtract, ALU.mult))
            op(V.tensor_tensor(S(LAM), S(LAM), S(LO), ALU.add))
            op(V.tensor_scalar(S(H2), S(H1), 1.0 / F, None, ALU.mult))
            op(V.tensor_scalar(XG[:], iota_f[:, 0:F], S(H2), S(LAM), ALU.mult, ALU.add))
            sturm(st2)
            op(V.tensor_scalar(cnt[:], cnt[:], iota_p[:], None, ALU.is_le))
            op(V.tensor_reduce(S(9), cnt[:], AX_X, ALU.add))
            op(V.tensor_scalar(S(9), S(9), 0.5, S(H2), ALU.subtract, ALU.mult))
            op(V.tensor_tensor(S(LAM), S(LAM), S(9), ALU.add))

            for l in range(LEVELS):
                op(V.tensor_copy(D4[:, l, :], dB[:] if l == 0 else D4[:, l - 1, :]))
                op(V.tensor_copy(EV[:, l, :], eB[:] if l == 0 else EV[:, l - 1, :]))
                op(V.tensor_copy(lam4[:, l:l + 1], S(LAM)))
                for c in (SPLITS[l - 1] if l else []):
                    op(V.tensor_scalar(D4[:, l, c - 1:c + 1], D4[:, l, c - 1:c + 1], M[0][:, c - 1:c], None,
                                       ALU.subtract))
                    op(V.memset(EV[:, l, c - 1:c], 0.0))
            op(V.tensor_tensor(E4[:], EV[:], EV[:], ALU.mult))
            op(V.tensor_scalar(E4[:], E4[:], TINY, -1.0, ALU.max, ALU.mult))
            op(V.memset(wrow[:], 0.0))
            for l in range(3):
                for c in SPLITS[l]:
                    op(V.memset(wrow[:, l, c - 1:c], 1.0))
                    op(V.tensor_scalar(wrow[:, l, c:c + 1], eB[:, c - 1:c], 0.0, -2.0, ALU.is_ge, ALU.mult))
                    op(V.tensor_scalar(wrow[:, l, c:c + 1], wrow[:, l, c:c + 1], 1.0, None, ALU.add))
                    op(V.tensor_scalar(wrow[:, 3 + l, c - 1:c + 1], M[0][:, c - 1:c].to_broadcast([N, 2]), 2.0 ** 0.5,
                                       None, ALU.mult))
            NE3 = NE[:].rearrange("p (i l) -> p i l", l=LANES)
            DM3 = PV[:, 0:N * LANES].rearrange("p (i l) -> p i l", l=LANES)
            RC3 = RC[:].rearrange("p (i l) -> p i l", l=LANES)
            op(V.memset(NE[:], 0.0))
            for l in range(LEVELS):
                op(V.tensor_copy(NE3[:, 1:N, l], E4[:, l, 0:N - 1]))
                op(V.tensor_copy(NE3[:, 1:N, LEVELS + l], E4[:, l, 0:N - 1][:, ::-1]))

            def twisted(sem, vectors):
                for l in range(LEVELS):
                    op(V.tensor_scalar(DM3[:, :, l], D4[:, l, :], lam4[:, l:l + 1], None, ALU.subtract))
                    op(V.tensor_scalar(DM3[:, :, LEVELS + l], D4[:, l, :][:, ::-1], lam4[:, l:l + 1], None,
                                       ALU.subtract))
                s = Tally(sem)
                for i in range(N - 1):
                    cur, nx = slice(i * LANES, (i + 1) * LANES), slice((i + 1) * LANES, (i + 2) * LANES)
                    s.did(V.reciprocal(RC[:, cur], PV[:, cur]))
                    s.last(dve)
                    s.did(V.tensor_tensor(r32[:, 0:LANES], RC[:, cur], NE[:, nx], ALU.mult))
                    s.last(dve)
                    s.did(V.tensor_tensor(PV[:, nx], r32[:, 0:LANES], PV[:, nx], ALU.add))
                    s.last(dve)
                op(V.reciprocal(RC[:, (N - 1) * LANES:], PV[:, (N - 1) * LANES:N * LANES]))
                op(V.tensor_scalar(RC[:], RC[:], 1e15, -1e15, ALU.min, ALU.max))
                for l in range(LEVELS):
                    qf, qb = DM3[:, :, l], DM3[:, :, LEVELS + l][:, ::-1]
                    rf, rb = RC3[:, :, l], RC3[:, :, LEVELS + l][:, ::-1]
                    op(V.scalar_tensor_tensor(out=M[3], in0=qb, scalar=lam4[:, l:l + 1], in1=qf,
                                              op0=ALU.add, op1=ALU.add))
                    op(V.tensor_tensor(M[3], M[3], D4[:, l, :], ALU.subtract))
                    op(V.scalar_tensor_tensor(out=M[4], in0=M[3], scalar=-1.0, in1=M[3], op0=ALU.mult, op1=ALU.max))
                    op(V.tensor_reduce(S(9), M[4], AX_X, ALU.min))
                    op(V.tensor_scalar(M[4], M[4], S(9), None, ALU.is_le))
                    total(S(9), M[3], M[4])
                    op(V.memset(M[5][:, 0:1], 0.0))
                    op(V.tensor_tensor(M[5][:, 1:N], EV[:, l, 0:N - 1], rb[:, 1:N], ALU.mult))
                    op(V.tensor_tensor_scan(M[6], M[5], M[4], 0.0, ALU.mult, ALU.add))
                    op(V.tensor_tensor(M[5], EV[:, l, :], rf, ALU.mult))
                    op(V.tensor_tensor_scan(M[7][:, ::-1], M[5][:, ::-1], M[4][:, ::-1], 0.0, ALU.mult, ALU.add))
                    op(V.tensor_tensor(M[6], M[6], M[7], ALU.add))
                    op(V.tensor_tensor(V4[:, l, :], M[6], M[4], ALU.subtract))
                    total(S(20 + l), V4[:, l, :], V4[:, l, :])
                    if not vectors:
                        op(V.reciprocal(S(29), S(20 + l)))
                        op(V.tensor_tensor(S(9), S(9), S(29), ALU.mult))
                        op(V.tensor_scalar(S(9), S(9), RAYLEIGH_CLIP, -RAYLEIGH_CLIP, ALU.min, ALU.max))
                        op(V.tensor_tensor(lam4[:, l:l + 1], lam4[:, l:l + 1], S(9), ALU.add))

            twisted(tw1, False)
            twisted(tw2, True)
            V.tensor_copy(S(41), S(20)).then_inc(rs_in, 1)
            dve.wait_ge(rs_out, 2)
            op(V.reciprocal(S(24, 4), S(24, 4)))
            for l in range(LEVELS):
                op(V.tensor_scalar(V4[:, l, :], V4[:, l, :], S(24 + l), None, ALU.mult))
            op(V.tensor_tensor(S(30), lam4[:, 0:1], ident[:, N - 1:N], ALU.mult))
            op(V.scalar_tensor_tensor(out=S(31), in0=ident[:, 64:65], scalar=wrow[:, 0, 64:65], in1=ident[:, 63:64],
                                      op0=ALU.mult, op1=ALU.add))
            ask(V.tensor_copy(S(42), S(30)))
            op(V.tensor_scalar(S(43), banks[6][:, 0:1], DEFLATE, None, ALU.mult))
            CC, ZZ, LF = 44, 47, 50
            for l in range(3):
                total(S(CC + l), V4[:, 0, :], wrow[:, l, :])
                op(V.scalar_tensor_tensor(out=M[3], in0=V4[:, l + 1, :], scalar=-1.0, in1=V4[:, l + 1, :],
                                          op0=ALU.mult, op1=ALU.max))
                total(S(ZZ + l), M[3], wrow[:, 3 + l, :])
                op(V.tensor_scalar(S(ZZ + l), S(ZZ + l), S(43), None, ALU.is_le))
            dve.wait_ge(leaf_sign, 1)
            op(V.tensor_scalar(S(LF), V4[:, 0, 0:1], sg[:, 0:1], -1.0, ALU.mult, ALU.mult))
            op(V.tensor_scalar(S(CC, 3), S(CC, 3), 0.0, None, ALU.is_lt))
            op(V.tensor_scalar(S(LF), S(LF), 0.0, None, ALU.is_lt))
            for l in (2, 1, 0):
                op(V.tensor_tensor(S(LF), S(LF), S(CC + l), ALU.subtract))
                op(V.scalar_tensor_tensor(out=S(LF), in0=S(LF), scalar=S(ZZ + l), in1=S(CC + l),
                                          op0=ALU.mult, op1=ALU.add))

            ask(V.tensor_copy(M[1], B[3]))
            op(V.tensor_copy(UT[:], B[3]))
            op(V.tensor_copy(S(32), banks[5][:, 0:1]))
            ask(V.tensor_copy(U[:], B[4]))
            for r in range(REFINES):
                if r:
                    ask(V.tensor_tensor(U[:], U[:], B[3], ALU.add))
                ask(V.tensor_copy(M[0], B[3]))
                op(V.tensor_copy(M[1], B[4]))
                op(V.tensor_copy(M[2], B[5]))
                total(S(51), M[1], I)
                total(S(52), M[2], I)
                op(V.reciprocal(S(52), S(52)))
                op(V.tensor_tensor(S(51), S(51), S(52), ALU.mult))
                ask(V.tensor_scalar(M[5], I, S(51), None, ALU.mult))
                op(V.tensor_scalar(M[3], B[6], S(51), None, ALU.subtract))
                op(V.tensor_tensor(M[4], I, M[2], ALU.subtract))
                op(V.tensor_tensor(M[6], M[4], B[6], ALU.mult))
                op(V.tensor_tensor(M[6], M[6], M[1], ALU.add))
                op(V.tensor_tensor(M[6], M[6], M[3], ALU.mult))
                op(V.scalar_tensor_tensor(out=M[6], in0=M[4], scalar=0.5 * REGULAR, in1=M[6],
                                          op0=ALU.mult, op1=ALU.add))
                op(V.tensor_tensor(M[3], M[3], M[3], ALU.mult))
                op(V.tensor_scalar(M[3], M[3], REGULAR, None, ALU.add))
                op(V.reciprocal(M[3], M[3]))
                ask(V.tensor_tensor(M[5], M[6], M[3], ALU.mult))
                op(V.tensor_tensor(UT[:], UT[:], B[4], ALU.add))
            ask(V.tensor_tensor(U[:], U[:], B[3], ALU.add))
            op(V.tensor_copy(S(53), banks[3][:, 0:1]))
            op(V.tensor_scalar(S(54), S(53), 0.0, None, ALU.is_lt))
            op(V.tensor_tensor(S(55), S(53), S(53), ALU.mult))
            op(V.tensor_scalar(S(55), S(55), 1e-8, None, ALU.is_gt))
            op(V.tensor_tensor(S(54), S(54), S(LF), ALU.subtract))
            op(V.scalar_tensor_tensor(out=S(54), in0=S(54), scalar=S(55), in1=S(LF), op0=ALU.mult, op1=ALU.add))
            op(V.tensor_scalar(S(54), S(54), 2.0, -1.0, ALU.mult, ALU.add))
            ask(V.tensor_scalar(UT[:], UT[:], S(54), None, ALU.mult))
            V.tensor_copy(U[:], B[4]).then_inc(eig_done, 1)
            dve.wait_ge(eig_done, 1)
            dve.wait_ge(w_kept, 2 * SKIPS + 3)

            def group(it, i):
                return bass.ds(it * (STREAMS * GB) + i * GB, GB)

            with V.Fori(0, ROUNDS) as it:
                for i in range(STREAMS):
                    dve.wait_ge(agg_ready[i], it + 1)
                    V.tensor_copy(mixS[i], bank[i][0]).then_inc(agg_kept[i], 1)
                for i in range(STREAMS):
                    dve.wait_ge(out_ready[i], it + 1)
                    V.tensor_tensor(batches(zS[i]), batches(bank[i][2]), b2B[:].unsqueeze(1).to_broadcast([N, GB, D]),
                                    ALU.add).then_inc(out_kept[i], 1)
                for i in range(STREAMS):
                    dve.wait_ge(back_ready[i], it + 1)
                    V.tensor_tensor(X[:, group(it, i), :], X[:, group(it, i), :], batches(bank[i][3]),
                                    ALU.add).then_inc(x1_ready[i], 1)
                for i in range(STREAMS):
                    dve.wait_ge(x1_ready[i], it + 1)
                    for b in range(GB):
                        at = bass.ds(it * (STREAMS * GB) + (i * GB + b), 1)
                        V.bn_stats(stats[:, at, :].rearrange("p b s -> p (b s)"),
                                   X[:, at, :].rearrange("p b d -> p (b d)")).then_inc(bn_done, 1)
            dve.wait_ge(bn_done, 2 * BATCH)
            deviations(2)
            for i in range(STREAMS):
                V.tensor_copy(sc[:, 56 + i:57 + i], sc[:, 62:63]).then_inc(sum_ready[i], 1)
            with V.Fori(0, ROUNDS) as it:
                for i in range(STREAMS):
                    dve.wait_ge(mix_ready[i], it + 1)
                    V.tensor_copy(mixS[i], bank[i][0]).then_inc(mix_kept[i], 1)
                for i in range(STREAMS):
                    dve.wait_ge(lin_ready[i], it + 1)
                    V.tensor_tensor(batches(linS[i]), batches(bank[i][1]), G0[:].unsqueeze(1).to_broadcast([N, GB, N]),
                                    ALU.add).then_inc(lin_kept[i], 1)
                for i in range(STREAMS):
                    dve.wait_ge(z_ready[i], it + 1)
                    V.tensor_tensor(batches(zS[i]), batches(bank[i][2]), bg1B[:].unsqueeze(1).to_broadcast([N, GB, D]),
                                    ALU.add).then_inc(z_kept[i], 1)
                for c, (p, j, b0, nb) in enumerate(CELLS):
                    W = N // p
                    T = nb * W
                    for i in range(STREAMS):
                        dve.wait_ge(acts_ready[i], it * len(CELLS) + c + 1)
                        if j == 0:
                            V.tensor_tensor(cS[i][:, 0:T], gI[i][:, 0:T], gG[i][:, 0:T], ALU.mult)\
                                .then_inc(cell_ready[i], 1)
                        else:
                            parts = it * PARTS + sum(2 for _, jj, _, _ in CELLS[:c] if jj)
                            V.tensor_tensor(gI[i][:, 0:T], gI[i][:, 0:T], gG[i][:, 0:T], ALU.mult).then_inc(cell_part[i], 1)
                            V.tensor_tensor(gF[i][:, 0:T], gF[i][:, 0:T], cS[i][:, 0:T], ALU.mult).then_inc(cell_part[i], 1)
                            dve.wait_ge(cell_part[i], parts + 2)
                            V.tensor_tensor(cS[i][:, 0:T], gI[i][:, 0:T], gF[i][:, 0:T], ALU.add)\
                                .then_inc(cell_ready[i], 1)
                    for i in range(STREAMS):
                        dve.wait_ge(tanh_ready[i], it * len(CELLS) + c + 1)
                        if j < p - 1:
                            dst = hS[i][:, 0:T].rearrange("p (b w) -> p b w", b=nb)
                        else:
                            dst = batches(HS[i])[:, b0:b0 + nb, p - 1:W * p:p]
                        V.tensor_tensor(dst, gO[i][:, 0:T].rearrange("p (b w) -> p b w", b=nb),
                                        tS[i][:, 0:T].rearrange("p (b w) -> p b w", b=nb),
                                        ALU.mult).then_inc(hidden_ready[i], 1)
                for i in range(STREAMS):
                    dve.wait_ge(turned_ready[i], it + 1)
                    V.tensor_tensor(X[:, group(it, i), :], X[:, group(it, i), :], batches(bank[i][0]),
                                    ALU.add).then_inc(sum_ready[i], 1)


_INS = ['x', 'adj', 'L0_gnn_W1', 'L0_gnn_b1', 'L0_gnn_W2', 'L0_gnn_b2', 'L1_gnn_Wg0', 'L1_gnn_bg0', 'L1_gnn_Wg1',
        'L1_gnn_bg1', 'L1_gnn_Wih', 'L1_gnn_Whh', 'L1_gnn_bih', 'L1_gnn_bhh']
_OUTS = [((BATCH, N, D), 'float32')]


def kernel(**inputs):
    import numpy as _np
    import concourse.bacc as _bacc
    from concourse import mybir as _mybir
    from concourse.bass_utils import run_bass_kernel_spmd as _run

    nc = _bacc.Bacc("TRN2", target_bir_lowering=False, num_devices=1)
    arrays, args = {}, {}
    for name in _INS:
        a = _np.ascontiguousarray(inputs[name])
        arrays[f"in_{name}"] = a
        args[name] = nc.dram_tensor(f"in_{name}", a.shape, _mybir.dt.from_np(a.dtype), kind="ExternalInput").ap()
    o = nc.dram_tensor("out_0", _OUTS[0][0], F32, kind="ExternalOutput").ap()
    build(nc, args, o)
    r = _run(nc, [arrays], core_ids=[0])
    return r.results[0]["out_0"]
```

```python
from contextlib import ExitStack

import concourse.bass as bass
from concourse import mybir

F32 = mybir.dt.float32
ALU = mybir.AluOpType
ACT = mybir.ActivationFunctionType
AX_X = mybir.AxisListType.X

N = 128
F = 16
LEAF = 16
LEVELS = 4
SPLITS = [[64], [32, 96], [16, 48, 80, 112]]
LANES = 2 * LEVELS
QR_SWEEPS = 16
DEFLATE = 8.0 * 2.0 ** -24
QR_EPS2 = (2.0 ** -24) ** 2
TINY = 1e-30
QR_PER = 97
RAYLEIGH_CLIP = 4e-5
REGULAR = 1e-12
REFINES = 2

BATCH, D = 128, 128
GB = 4
STREAMS = 4
ROUNDS = BATCH // (GB * STREAMS)
GW = GB * D
SKIPS = 4
LN_EPS = 1e-5
GATE_I, GATE_F, GATE_G, GATE_O = range(4)
TWIST = N // 2
HALF = GW // 2
CELLS = [(1, 0, 0, GB // 2), (1, 0, GB // 2, GB // 2)] + [(p, j, 0, GB) for p in range(2, SKIPS + 1) for j in range(p)]


class Tally:

    def __init__(self, sem, base=0):
        self.sem, self.base, self.n = sem, base, 0

    def did(self, ins):
        ins.then_inc(self.sem, 1)
        self.n += 1
        return self.n

    def last(self, eng):
        eng.wait_ge(self.sem, self.base + self.n)


def build(nc, t_in, out):
    with ExitStack() as ctx:
        def sb(name, shape, dt=F32):
            return ctx.enter_context(nc.sbuf_tensor(name, shape, dt))

        def sem(name):
            return ctx.enter_context(nc.semaphore(name))

        banks = [ctx.enter_context(nc.psum_tensor(f"bank{i}", [128, 512], F32)) for i in range(8)]
        adj = sb("adj", [N, N])
        ident = sb("ident", [N, N + 1])
        ones = sb("ones", [N, N])
        below = sb("below", [N, N + 1])
        iota_f = sb("iota_f", [N, N])
        iota_p = sb("iota_p", [N, 1])
        grid = sb("grid", [N, F])
        Lap = sb("Lap", [N, N])
        A = sb("A", [N, N])
        uB = sb("uB", [N, 2, N])
        u_c = sb("u_c", [N, 1])
        wB = sb("wB", [N, N])
        sc = sb("sc", [N, 64])
        scp = sb("scp", [N, 64])
        Um = sb("Um", [N, N])
        hB = sb("hB", [N, N])
        eB = sb("eB", [N, N])
        dB = sb("dB", [N, N])
        m = [sb(f"m{i}", [N, N]) for i in range(10)]
        PV = sb("PV", [N, 8 * GW])
        RC = sb("RC", [N, N * LANES])
        BIG = sb("BIG", [N, 8 * GW])
        leaf = sb("leaf", [N, 8 * LEAF + 64])
        leaf3 = sb("leaf3", [N, 10 * LEAF])
        leaf2 = sb("leaf2", [N, 7 * LEAF])
        U = sb("U", [N, N])
        UT = sb("UT", [N, N])
        QT = sb("QT", [N, N])
        cnt = sb("cnt", [N, F])
        XG = sb("XG", [N, F])
        r32 = sb("r32", [N, F])
        r32b = sb("r32b", [N, F])
        D4 = sb("D4", [N, LEVELS, N])
        EV = sb("EV", [N, LEVELS, N])
        wrow = sb("wrow", [N, 6, N])
        V4 = sb("V4", [N, LEVELS, N])
        lam4 = sb("lam4", [N, LEVELS])

        X = sb("X", [N, BATCH, D])
        stats = sb("stats", [N, BATCH, 6])
        ln = sb("ln", [N, 4, BATCH])
        wT = sb("wT", [N, 2, SKIPS, 4 * D])
        adjT = sb("adjT", [N, N])
        bias_nat = sb("bias_nat", [4 * SKIPS, 2, D])
        ahead = sb("ahead", [N, STREAMS * GW])
        act_scratch = sb("act_scratch", [N, 1])
        bias = sb("bias", [N, 4 * SKIPS])
        W1, W2, Wg0, Wg1 = sb("W1", [N, D]), sb("W2", [N, D]), sb("Wg0", [N, D]), sb("Wg1", [N, D])
        b1 = sb("b1", [N, 1])
        b2B, bg0B, bg1B = sb("b2B", [N, D]), sb("bg0B", [N, D]), sb("bg1B", [N, D])
        G0 = sb("G0", [N, N])
        spare = sb("spare", [N, 16 * GW])
        w_nat = spare[:, 0:2 * SKIPS * 4 * D].rearrange("n (c p g h) -> n c p g h", c=2, p=SKIPS, g=4)

        X_CHUNKS = 4
        x_in = [sem(f"x_in{c}") for c in range(X_CHUNKS)]
        tables = sem("tables")
        weights_in = sem("weights_in")
        small_in = sem("small_in")
        w_turned = sem("w_turned")
        w_kept = sem("w_kept")
        small_turned = sem("small_turned")
        ln_var = sem("ln_var")
        ln_dev = sem("ln_dev")
        ln_done = sem("ln_done")
        eig_done = sem("eig_done")

        def per_stream(name):
            return [sem(f"{name}{i}") for i in range(STREAMS)]

        h_ready, agg_ready, agg_kept, hid_ready, relu_ready = map(per_stream, ("h", "agg", "aggk", "hid", "relu"))
        out_ready, out_kept, back_ready, x1_ready = map(per_stream, ("o", "ok", "back", "x1"))
        h1_ready, mix_ready, mix_kept, lin_ready, lin_kept = map(per_stream, ("h1", "mix", "mixk", "lin", "link"))
        y_ready, z_ready, z_kept, conv_ready, H_ready = map(per_stream, ("y", "z", "zk", "conv", "H"))
        gates_ready, acts_ready, cell_part, cell_ready = map(per_stream, ("gates", "acts", "cellp", "cell"))
        tanh_ready, hidden_ready, turned_ready, sum_ready = map(per_stream, ("tanh", "hidden", "turned", "sum"))

        bn_done = sem("bn_done")
        PARTS = sum(2 for _, j, _, _ in CELLS if j)
        TURNS = [(c, i) for c in range(len(CELLS)) for i in range(STREAMS)]
        adj_in = sem("adj_in")
        consts = sem("consts")
        v_ = sem("v_")
        hv = sem("hv")
        x_ready = sem("x_ready")
        xb_ready = sem("xb_ready")
        sign_ready = sem("sign_ready")
        row_ready = sem("row_ready")
        pb_ready = sem("pb_ready")
        sigma_ready = sem("sigma_ready")
        u_ready = sem("u_ready")
        um_kept = sem("um_kept")
        p_ready = sem("p_ready")
        a_ready = sem("a_ready")
        leaf_ready = sem("leaf_ready")
        leaf_sign = sem("leaf_sign")
        to_pe = sem("to_pe")
        from_pe = sem("from_pe")
        rs_in = sem("rs_in")
        rs_out = sem("rs_out")
        st1, st2, tw1, tw2 = sem("st1"), sem("st2"), sem("tw1"), sem("tw2")
        pool_s = sem("pool_s")
        pool_q = sem("pool_q")
        stv = sem("stv")
        stored = sem("stored")
        block = ctx.enter_context(nc.Block())

        STEPS = N - 1

        d16, e16 = leaf[:, 0:16], leaf[:, 16:32]
        am = leaf[:, 32:48]
        tmp = leaf[:, 48:64]
        oh = leaf[:, 64:80]
        runs = [leaf2[:, 0:32], leaf2[:, 32:64]]
        pick = leaf2[:, 64:112].rearrange("p (c f) -> p c f", f=LEAF)
        sg = leaf[:, 96:160]
        pi, rho, w16, we, y16, ey, c16, gam, ne16, neg16 = (leaf3[:, c * LEAF:(c + 1) * LEAF] for c in range(10))

        pieces = [BIG[:, c * GW:(c + 1) * GW] for c in range(8)] + [PV[:, c * GW:(c + 1) * GW] for c in range(8)] \
            + [spare[:, c * GW:(c + 1) * GW] for c in range(16)]
        gI, gF, gG, gO, cS, HS, tS, hS = ([pieces[STREAMS * c + i] for i in range(STREAMS)] for c in range(8))
        hs = [ahead[:, i * GW:(i + 1) * GW] for i in range(STREAMS)]
        gate_out = {GATE_I: gI, GATE_G: gG, GATE_F: gF, GATE_O: gO}
        mixS, linS, yS, zS = gF, gG, gO, cS

        def batches(v):
            return v.rearrange("p (b t) -> p b t", b=GB)

        bank = [[banks[2 * i + c % 2][:] for c in range(4)] for i in range(STREAMS)]

        def gate(i, q, T):
            return banks[2 * i + (q in (GATE_F, GATE_O))][:, HALF * (q in (GATE_G, GATE_O)):][:, 0:T]
        x_dram = t_in["x"].rearrange("b n d -> n b d")
        out_dram = out.rearrange("b n d -> n b d")
        BN_LAG = 16

        @block.sync
        def _(sp):
            sp.dma_start(adj[:], t_in["adj"]).then_inc(adj_in, 16)
            for c in range(X_CHUNKS):
                r = slice(c * BATCH // X_CHUNKS, (c + 1) * BATCH // X_CHUNKS)
                sp.dma_start(X[:, r, :], x_dram[:, r, :]).then_inc(x_in[c], 16)
            for c, name in enumerate(("L1_gnn_Wih", "L1_gnn_Whh")):
                for p in range(SKIPS):
                    sp.dma_start(w_nat[:, c, p], t_in[name][p].rearrange("(g u) h -> u g h", g=4)).then_inc(weights_in, 16)
            for t, name in ((W1, "L0_gnn_W1"), (W2, "L0_gnn_W2"), (Wg0, "L1_gnn_Wg0"), (Wg1, "L1_gnn_Wg1")):
                sp.dma_start(t[:], t_in[name]).then_inc(small_in, 16)
            for t, name in ((b2B, "L0_gnn_b2"), (bg0B, "L1_gnn_bg0"), (bg1B, "L1_gnn_bg1")):
                sp.dma_start(t[:], t_in[name].rearrange("(a d) -> a d", a=1).to_broadcast([N, D])).then_inc(small_in, 16)
            sp.dma_start(b1[:], t_in["L0_gnn_b1"].rearrange("(d a) -> d a", a=1)).then_inc(small_in, 16)
            for c, name in enumerate(("L1_gnn_bih", "L1_gnn_bhh")):
                sp.dma_start(bias_nat[:, c, :], t_in[name].rearrange("p (g u) -> (p g) u", g=4)).then_inc(small_in, 16)
            with nc.sync.Fori(0, ROUNDS) as it:
                for i in range(STREAMS):
                    b = bass.ds(it * (STREAMS * GB) + i * GB, GB)
                    sp.wait_ge(sum_ready[i], it + 1)
                    sp.dma_start(out_dram[:, b, :], X[:, b, :]).then_inc(stored, 16)
            sp.wait_ge(stored, 16 * ROUNDS * STREAMS)

        @block.gpsimd
        def _(pool):
            p = Tally(consts)
            nc.gpsimd.memset(ones[:], 1.0).then_inc(pool_s, 1)
            pool.wait_ge(pool_s, 1)
            p.did(nc.gpsimd.affine_select(out=ident[:, 0:N], in_=ones[:], compare_op=ALU.is_equal, fill=0.0,
                                          base=0, pattern=[[-1, N]], channel_multiplier=1))
            p.did(nc.gpsimd.affine_select(out=below[:, 0:N], in_=ones[:], compare_op=ALU.is_gt, fill=0.0,
                                          base=0, pattern=[[-1, N]], channel_multiplier=1))
            p.did(nc.gpsimd.iota(iota_f[:], pattern=[[1, N]], base=0, channel_multiplier=0,
                                 allow_small_or_imprecise_dtypes=True))
            p.did(nc.gpsimd.iota(iota_p[:], pattern=[[1, 1]], base=0, channel_multiplier=1,
                                 allow_small_or_imprecise_dtypes=True))
            p.did(nc.gpsimd.iota(grid[:], pattern=[[1, F]], base=0, channel_multiplier=F,
                                 allow_small_or_imprecise_dtypes=True))
            p.did(nc.gpsimd.memset(leaf2[:], 1.0))
            p.did(nc.gpsimd.memset(sg, 1.0))
            pool.wait_ge(consts, 7)

            pool.wait_ge(leaf_ready, 1)
            S = lambda i, n=1: sg[:, i:i + n]
            PAR, NEG1, HALF, T0, R_, P_, SIG, OG = 0, 2, 4, 10, 12, 14, 16, 18
            q = Tally(pool_q)

            def op(ins):
                q.did(ins)
                q.last(pool)

            op(nc.gpsimd.memset(S(NEG1, 2), -1.0))
            op(nc.gpsimd.memset(S(HALF, 2), 0.5))
            op(nc.gpsimd.memset(leaf3[:], 1.0))
            op(nc.gpsimd.memset(neg16, -1.0))
            TT = nc.gpsimd.tensor_tensor
            TS = nc.gpsimd.tensor_scalar
            with nc.gpsimd.Fori(0, QR_SWEEPS) as k:
                pool.sem_clear(pool_q)
                q = Tally(pool_q)

                def op(ins):
                    q.did(ins)
                    q.last(pool)
                op(TT(tmp[:, 0:15], d16[:, 0:15], d16[:, 1:16], ALU.mult))
                op(TS(tmp[:, 0:15], tmp[:, 0:15], QR_EPS2, None, ALU.mult))
                op(TT(tmp[:, 0:15], e16[:, 0:15], tmp[:, 0:15], ALU.subtract))
                op(TS(tmp[:, 0:15], tmp[:, 0:15], 0.0, None, ALU.is_gt))
                op(TT(e16[:, 0:15], e16[:, 0:15], tmp[:, 0:15], ALU.mult))
                op(TS(runs[0][:, 0:14], tmp[:, 1:15], -1.0, 1.0, ALU.mult, ALU.add))
                for c in range(4):
                    op(TT(runs[(c + 1) % 2][:, 0:LEAF], runs[c % 2][:, 0:LEAF],
                          runs[c % 2][:, 2 ** c:LEAF + 2 ** c], ALU.mult))
                op(TT(oh[:, 0:15], runs[0][:, 0:15], tmp[:, 0:15], ALU.mult))
                for c, v in enumerate((d16[:, 1:16], d16[:, 0:15], e16[:, 0:15])):
                    op(TT(pick[:, c, 0:15], v, oh[:, 0:15], ALU.mult))
                op(nc.gpsimd.memset(pick[:, :, 15:16], 0.0))
                for w in (8, 4, 2, 1):
                    op(TT(pick[:, :, 0:w], pick[:, :, 0:w], pick[:, :, w:2 * w], ALU.add))
                op(nc.gpsimd.tensor_copy(S(SIG), pick[:, 0, 0:1]))
                op(nc.gpsimd.tensor_copy(S(T0), pick[:, 1, 0:1]))
                op(nc.gpsimd.tensor_copy(S(R_), pick[:, 2, 0:1]))
                op(TS(S(T0), S(T0), S(SIG), 0.5, ALU.subtract, ALU.mult))
                op(TT(S(P_), S(T0), S(T0), ALU.mult))
                op(TS(S(P_), S(P_), S(R_), TINY, ALU.add, ALU.add))
                op(TT(S(P_), S(P_), S(HALF), ALU.pow))
                op(TS(S(OG), S(T0), 0.0, 2.0, ALU.is_ge, ALU.mult))
                op(TS(S(OG), S(OG), 1.0, S(P_), ALU.subtract, ALU.mult))
                op(TT(S(OG), S(OG), S(T0), ALU.add))
                op(TT(S(OG), S(OG), S(NEG1), ALU.pow))
                op(TT(S(OG), S(OG), S(R_), ALU.mult))
                op(TT(S(SIG), S(SIG), S(OG), ALU.subtract))
                op(TS(am, d16, S(SIG), 1e-15, ALU.subtract, ALU.add))
                op(TS(S(T0), am[:, 0:1], 0.0, -2.0, ALU.is_ge, ALU.mult))
                op(TS(S(PAR), S(T0), 1.0, S(PAR), ALU.add, ALU.mult))
                op(TS(ne16, e16, -1.0, None, ALU.mult))
                op(nc.gpsimd.tensor_copy(pi[:, 0:1], am[:, 0:1]))
                op(TT(rho[:, 0:1], pi[:, 0:1], neg16[:, 0:1], ALU.pow))
                for i in range(LEAF - 1):
                    op(TS(pi[:, i + 1:i + 2], rho[:, i:i + 1], ne16[:, i:i + 1], am[:, i + 1:i + 2],
                          ALU.mult, ALU.add))
                    op(TT(rho[:, i + 1:i + 2], pi[:, i + 1:i + 2], neg16[:, 0:1], ALU.pow))
                op(TT(w16, rho, rho, ALU.mult))
                op(TT(we[:, 1:LEAF], w16[:, 1:LEAF], e16[:, 0:LEAF - 1], ALU.mult))
                op(nc.gpsimd.tensor_copy(y16[:, 0:1], w16[:, 0:1]))
                for i in range(1, LEAF):
                    op(TS(y16[:, i:i + 1], y16[:, i - 1:i], we[:, i:i + 1], w16[:, i:i + 1], ALU.mult, ALU.add))
                op(TT(ey[:, 0:LEAF], e16, y16, ALU.mult))
                op(TS(c16[:, 1:LEAF], ey[:, 0:LEAF - 1], 1.0, None, ALU.add))
                op(TT(c16[:, 1:LEAF], c16[:, 1:LEAF], neg16[:, 1:LEAF], ALU.pow))
                op(TT(ey[:, 0:LEAF - 1], ey[:, 0:LEAF - 1], c16[:, 1:LEAF], ALU.mult))
                op(TT(gam, c16, pi, ALU.mult))
                op(TT(y16, y16, neg16, ALU.pow))
                op(TT(y16, y16, e16, ALU.add))
                op(TT(e16[:, 0:LEAF - 1], ey[:, 0:LEAF - 1], y16[:, 1:LEAF], ALU.mult))
                op(TT(d16[:, 0:LEAF - 1], d16[:, 1:LEAF], gam[:, 0:LEAF - 1], ALU.add))
                op(TT(d16[:, 0:LEAF - 1], d16[:, 0:LEAF - 1], gam[:, 1:LEAF], ALU.subtract))
                op(TT(d16[:, LEAF - 1:LEAF], S(SIG), gam[:, LEAF - 1:LEAF], ALU.add))
                assert q.n == QR_PER, q.n
            nc.gpsimd.tensor_copy(S(PAR), S(PAR)).then_inc(leaf_sign, 1)

        @block.scalar
        def _(act):
            act.wait_ge(rs_in, 1)
            nc.scalar.activation(m[5][:], m[4][:], ACT.Sqrt).then_inc(rs_out, 1)
            for k in range(STEPS):
                act.wait_ge(xb_ready, k + 1)
                nc.scalar.activation(sc[:, 0:1], banks[0][:, N:N + 1], ACT.Sqrt).then_inc(sigma_ready, 1)
                act.wait_ge(sign_ready, k + 1)
                nc.scalar.activation(uB[:, k % 2], banks[0][:, 0:N], ACT.Copy).then_inc(row_ready, 1)
                act.wait_ge(u_ready, k + 1)
                nc.scalar.activation(Um[:, k:k + 1], u_c[:], ACT.Copy).then_inc(um_kept, 1)
            for c in range(2 * SKIPS):
                act.wait_ge(w_turned, c + 1)
                nc.scalar.activation(wT[:, c // SKIPS, c % SKIPS, :], banks[c % 2][:], ACT.Copy).then_inc(w_kept, 1)
            act.wait_ge(small_turned, 1)
            nc.scalar.activation(adjT[:], banks[0][:, 0:N], ACT.Copy).then_inc(w_kept, 1)
            nc.scalar.activation(bias[:], banks[0][:, N:N + 4 * SKIPS], ACT.Copy).then_inc(w_kept, 1)
            act.wait_ge(small_turned, 2)
            nc.scalar.activation(G0[:], banks[1][:, 0:N], ACT.Copy).then_inc(w_kept, 1)
            act.wait_ge(ln_var, 1)
            nc.scalar.activation(ln[:, 2, :], ln[:, 1, :], ACT.Sqrt).then_inc(ln_dev, 1)
            act.wait_ge(rs_in, 2)
            nc.scalar.activation(sc[:, 24:28], sc[:, 20:24], ACT.Sqrt).then_inc(rs_out, 1)

            def batch(it, i, b):
                return it * (STREAMS * GB) + (i * GB + b)

            def normalize(it, i, b, done):
                at = bass.ds(batch(it, i, b), 1)
                ins = nc.scalar.activation(hs[i][:, b * D:(b + 1) * D], X[:, at, :].rearrange("p b d -> p (b d)"),
                                           ACT.Relu, bias=ln[:, 3, at], scale=ln[:, 2, at])
                if b == GB - 1:
                    ins.then_inc(done[i], 1)

            def first_layer(it, more):
                for i in range(STREAMS):
                    act.wait_ge(hid_ready[i], it + 1)
                    nc.scalar.activation(linS[i], bank[i][1], ACT.Relu, bias=b1[:, 0:1]).then_inc(relu_ready[i], 1)
                if more:
                    for i in range(STREAMS):
                        for b in range(GB):
                            normalize(it + 1, i, b, h_ready)

            act.wait_ge(ln_done, 1)
            for i in range(STREAMS):
                for b in range(GB):
                    normalize(0, i, b, h_ready)
            with nc.scalar.Fori(0, ROUNDS - 1) as it:
                first_layer(it, True)
            first_layer(ROUNDS - 1, False)

            act.wait_ge(ln_var, 2)
            nc.scalar.activation(ln[:, 2, :], ln[:, 1, :], ACT.Sqrt).then_inc(ln_dev, 1)
            act.wait_ge(ln_done, 2)
            nc.scalar.activation(act_scratch[:], ln[:, 2, 0:1], ACT.Sigmoid).then_inc(tables, 1)
            for i in range(STREAMS):
                for b in range(GB):
                    normalize(0, i, b, h1_ready)

            def gates(it, c, i, qs):
                p, j, _, nb = CELLS[c]
                T = nb * (N // p)
                for q in qs:
                    if q == GATE_F and j == 0:
                        continue
                    at = (p - 1) * 4 + q
                    last = nc.scalar.activation(gate_out[q][i][:, 0:T], gate(i, q, T),
                                                ACT.Tanh if q == GATE_G else ACT.Sigmoid, bias=bias[:, at:at + 1])
                if q == GATE_F:
                    last.then_inc(acts_ready[i], 1)

            def cell_tanh(it, c, i):
                p, _, _, nb = CELLS[c]
                T = nb * (N // p)
                act.wait_ge(cell_ready[i], it * len(CELLS) + c + 1)
                nc.scalar.activation(tS[i][:, 0:T], cS[i][:, 0:T], ACT.Tanh).then_inc(tanh_ready[i], 1)

            def second_layer(it, more):
                act.wait_ge(tables, it + 1)
                nc.scalar.activation(act_scratch[:], ln[:, 2, 0:1], ACT.Sigmoid).then_inc(tables, 1)
                for i in range(STREAMS):
                    act.wait_ge(lin_kept[i], it + 1)
                    nc.scalar.activation(yS[i], linS[i], ACT.Relu).then_inc(y_ready[i], 1)
                for i in range(STREAMS):
                    act.wait_ge(conv_ready[i], it + 1)
                    nc.scalar.activation(HS[i], bank[i][0], ACT.Relu).then_inc(H_ready[i], 1)
                todo = [(i, b) for i in range(STREAMS) for b in range(GB)] if more else []
                for n, (c, i) in enumerate(TURNS):
                    act.wait_ge(gates_ready[i], it * len(CELLS) + c + 1)
                    gates(it, c, i, (GATE_I, GATE_G, GATE_F))
                    if n:
                        cell_tanh(it, *TURNS[n - 1])
                    gates(it, c, i, (GATE_O,))
                    if todo and n % 2:
                        normalize(it + 1, *todo.pop(0), h1_ready)
                cell_tanh(it, *TURNS[-1])

            with nc.scalar.Fori(0, ROUNDS - 1) as it:
                second_layer(it, True)
            second_layer(ROUNDS - 1, False)

        B = [b[:, 0:N] for b in banks]
        M = [x[:] for x in m]

        @block.tensor
        def _(pe):
            n = [0]

            def mms(*jobs):
                n[0] += 1
                pe.wait_ge(to_pe, n[0])
                for j in jobs:
                    if len(j) == 2:
                        last = nc.tensor.transpose(j[0], j[1], ident[:, 0:N])
                    else:
                        last = nc.tensor.matmul(j[0], j[1], j[2], start=True, stop=True)
                last.then_inc(from_pe, 1)

            def householder(k):
                pe.wait_ge(x_ready, k + 1)
                nc.tensor.matmul(banks[0][:, 0:N + 1], ident[:, N:N + 1].to_broadcast([N, N]), ident[:, 0:N + 1],
                                 start=True, stop=True).then_inc(xb_ready, 1)
                pe.wait_ge(u_ready, k + 1)
                pe.wait_ge(a_ready, k + 1)
                nc.tensor.matmul(B[1], u_c[:].to_broadcast([N, N]), A[:], start=True, stop=True).then_inc(pb_ready, 1)
                nc.tensor.matmul(banks[2][:, 0:1], A[:], u_c[:], start=True, stop=True).then_inc(p_ready, 1)

            mms((B[3], ones[:], M[0]))
            mms((B[3], M[6]))
            for k in range(LEAF):
                householder(k)
            mms((B[3], ones[:], M[2]))
            for k in range(LEAF, STEPS):
                householder(k)
            mms((B[3], ones[:], M[2]), (B[4], Um[:], Um[:]))
            mms((B[3], M[1]), (B[4], Um[:]))
            mms((B[3], M[1], M[0]), (B[4], M[0], M[1]))
            for r in range(6):
                if r < 5:
                    mms((B[5], M[4], M[6]), (B[3], M[4], M[3]), (B[4], M[3], M[4]))
                else:
                    mms((B[5], M[4], M[6]))
            mms((B[3], M[7], M[8]))
            mms((B[3], M[8], M[5]))
            pe.wait_ge(weights_in, 16 * 2 * SKIPS)
            for c in range(2 * SKIPS):
                if c >= 2:
                    pe.wait_ge(w_kept, c - 1)
                for q in range(4):
                    last = nc.tensor.transpose(banks[c % 2][:, q * D:(q + 1) * D], w_nat[:, c // SKIPS, c % SKIPS, q, :],
                                               ident[:, 0:N])
                last.then_inc(w_turned, 1)
            pe.wait_ge(small_in, 16 * 10)
            pe.wait_ge(w_kept, 2 * SKIPS)
            nc.tensor.transpose(banks[0][:, 0:N], adj[:], ident[:, 0:N])
            K = 4 * SKIPS
            nc.tensor.matmul(banks[0][:, N:N + K], bias_nat[:, 0, :], ident[0:K, 0:K], start=True, stop=False)
            nc.tensor.matmul(banks[0][:, N:N + K], bias_nat[:, 1, :], ident[0:K, 0:K],
                             start=False, stop=True).then_inc(small_turned, 1)
            pe.wait_ge(w_kept, 2 * SKIPS + 2)
            nc.tensor.matmul(banks[1][:, 0:N], bg0B[:], adjT[:], start=True, stop=True).then_inc(small_turned, 1)
            for f in range(F):
                pe.wait_ge(stv, f + 1)
                ins = nc.tensor.matmul(banks[6][:, 0:1], BIG[:, f * N:(f + 1) * N], ones[:, 0:1],
                                       start=(f == 0), stop=(f == F - 1))
            ins.then_inc(from_pe, 1)
            mms((B[3], V4[:, 0, :]), (banks[6][:, 0:1], sc[:, 30:31].to_broadcast([N, N]), ones[:, 0:1]))
            mms((B[3], M[1], QT[:]), (B[4], QT[:], M[1]), (banks[5][:, 0:1], QT[:], sc[:, 31:32]))
            for r in range(REFINES):
                mms((B[3], Lap[:], U[:]))
                mms((B[4], U[:], M[0]), (B[5], U[:], U[:]))
                mms((B[6], ones[:], M[5]))
                mms((B[3], UT[:], M[5]), (B[4], M[5], UT[:]))
            mms((banks[3][:, 0:1], U[:], sc[:, 32:33]))
            mms((B[4], UT[:]))

            pe.wait_ge(eig_done, 1)
            with nc.tensor.Fori(0, ROUNDS) as it:
                for i in range(STREAMS):
                    pe.wait_ge(h_ready[i], it + 1)
                    for b in range(GB):
                        last = nc.tensor.matmul(bank[i][0][:, b * N:(b + 1) * N], hs[i][:, b * D:(b + 1) * D], U[:],
                                                start=True, stop=True)
                    last.then_inc(agg_ready[i], 1)
                for i in range(STREAMS):
                    pe.wait_ge(agg_kept[i], it + 1)
                    nc.tensor.matmul(bank[i][1], W1[:], mixS[i], start=True, stop=True).then_inc(hid_ready[i], 1)
                for i in range(STREAMS):
                    pe.wait_ge(relu_ready[i], it + 1)
                    for b in range(GB):
                        last = nc.tensor.matmul(bank[i][2][:, b * D:(b + 1) * D], linS[i][:, b * N:(b + 1) * N], W2[:],
                                                start=True, stop=True)
                    last.then_inc(out_ready[i], 1)
                for i in range(STREAMS):
                    pe.wait_ge(out_kept[i], it + 1)
                    nc.tensor.matmul(bank[i][3], UT[:], zS[i], start=True, stop=True).then_inc(back_ready[i], 1)

            def mix(it, i):
                pe.wait_ge(h1_ready[i], it + 1)
                for b in range(GB):
                    last = nc.tensor.matmul(bank[i][0][:, b * N:(b + 1) * N], hs[i][:, b * D:(b + 1) * D], adjT[:],
                                            start=True, stop=True)
                last.then_inc(mix_ready[i], 1)

            def turn_back(it, i):
                pe.wait_ge(hidden_ready[i], it * len(CELLS) + len(CELLS))
                for b in range(GB):
                    last = nc.tensor.transpose(bank[i][1][:, b * D:(b + 1) * D], HS[i][:, b * N:(b + 1) * N],
                                               ident[:, 0:N])
                last.then_inc(turned_ready[i], 1)

            def second_layer(it):
                for i in range(STREAMS):
                    pe.wait_ge(mix_kept[i], it + 1)
                    nc.tensor.matmul(bank[i][2], Wg0[:], mixS[i], start=True, stop=True).then_inc(lin_ready[i], 1)
                for i in range(STREAMS):
                    pe.wait_ge(y_ready[i], it + 1)
                    for b in range(GB):
                        last = nc.tensor.matmul(bank[i][3][:, b * D:(b + 1) * D], yS[i][:, b * N:(b + 1) * N], Wg1[:],
                                                start=True, stop=True)
                    last.then_inc(z_ready[i], 1)
                for i in range(STREAMS):
                    pe.wait_ge(z_kept[i], it + 1)
                    for b in range(GB):
                        last = nc.tensor.matmul(bank[i][0][:, b * N:(b + 1) * N], zS[i][:, b * D:(b + 1) * D], adjT[:],
                                                start=True, stop=True)
                    last.then_inc(conv_ready[i], 1)
                for c, (p, j, b0, nb) in enumerate(CELLS):
                    W = N // p
                    for i in range(STREAMS):
                        todo = [q for q in (GATE_I, GATE_G, GATE_F, GATE_O) if j or q != GATE_F]
                        xt = batches(HS[i])[:, b0:b0 + nb, j:(W - 1) * p + j + 1:p]
                        if c == 0:
                            pe.wait_ge(H_ready[i], it + 1)
                        elif j == 0:
                            pe.wait_ge(hidden_ready[i], it * len(CELLS) + c)
                        else:
                            pe.wait_ge(tanh_ready[i], it * len(CELLS) + c)
                        early = [q for q in todo if q in (GATE_I, GATE_F)]
                        for q in early:
                            last = nc.tensor.matmul(gate(i, q, nb * W), wT[:, 0, p - 1, q * D:(q + 1) * D], xt,
                                                    start=True, stop=(j == 0))
                        if j:
                            pe.wait_ge(hidden_ready[i], it * len(CELLS) + c)
                            for q in early:
                                last = nc.tensor.matmul(gate(i, q, nb * W), wT[:, 1, p - 1, q * D:(q + 1) * D],
                                                        hS[i][:, 0:GB * W], start=False, stop=True)
                        for q in todo:
                            if q in early:
                                continue
                            last = nc.tensor.matmul(gate(i, q, nb * W), wT[:, 0, p - 1, q * D:(q + 1) * D], xt,
                                                    start=True, stop=(j == 0))
                            if j:
                                last = nc.tensor.matmul(gate(i, q, nb * W), wT[:, 1, p - 1, q * D:(q + 1) * D],
                                                        hS[i][:, 0:GB * W], start=False, stop=True)
                        last.then_inc(gates_ready[i], 1)

            for i in range(STREAMS):
                mix(0, i)
            with nc.tensor.Fori(0, ROUNDS - 1) as it:
                second_layer(it)
                for i in range(STREAMS - 1):
                    turn_back(it, i)
                for i in range(STREAMS - 1):
                    mix(it + 1, i)
                turn_back(it, STREAMS - 1)
                mix(it + 1, STREAMS - 1)
            second_layer(ROUNDS - 1)
            for i in range(STREAMS):
                turn_back(ROUNDS - 1, i)

        @block.vector
        def _(dve):
            t = Tally(v_)
            V = nc.vector
            asked, answered = [0], [0]

            def op(ins):
                t.did(ins)
                t.last(dve)

            def ask(ins):
                ins.then_inc(to_pe, 1)
                asked[0] += 1
                answered[0] += 1
                dve.wait_ge(from_pe, answered[0])

            def S(i, n=1):
                return sc[:, i:i + n]

            def total(dst, a, b, alu=ALU.add, junk=None):
                op(V.tensor_tensor_reduce(out=(m[9][:] if junk is None else junk), in0=a, in1=b, scale=1.0, scalar=0.0,
                                          op0=ALU.mult, op1=alu, accum_out=dst))

            I = ident[:, 0:N]
            op(V.memset(sc[:], 0.0))
            op(V.memset(eB[:], 0.0))
            op(V.memset(hB[:], 0.0))
            op(V.memset(Um[:], 0.0))
            dve.wait_ge(adj_in, 16)
            dve.wait_ge(consts, 7)
            op(V.tensor_reduce(S(1), adj[:], AX_X, ALU.add))
            total(S(2), adj[:], I)
            op(V.tensor_tensor(S(3), S(1), S(2), ALU.subtract))
            ask(V.scalar_tensor_tensor(out=M[0], in0=I, scalar=S(3), in1=adj[:], op0=ALU.mult, op1=ALU.add))
            op(V.tensor_copy(M[1], B[3]))
            op(V.tensor_scalar(M[3], M[1], 0.0, None, ALU.is_gt))
            V.tensor_scalar(M[4], M[1], TINY, None, ALU.max).then_inc(rs_in, 1)
            dve.wait_ge(rs_in, 1)
            dve.wait_ge(rs_out, 1)
            op(V.reciprocal(M[5], M[5]))
            op(V.tensor_tensor(M[2], M[5], M[5], ALU.mult))
            op(V.tensor_tensor(M[2], M[2], M[4], ALU.mult))
            op(V.tensor_scalar(M[2], M[2], -0.5, 1.5, ALU.mult, ALU.add))
            op(V.tensor_tensor(M[2], M[2], M[5], ALU.mult))
            op(V.tensor_tensor(M[4], M[2], M[3], ALU.mult))
            total(S(7), M[4], I)
            op(V.tensor_tensor(M[5], M[1], I, ALU.mult))
            op(V.tensor_tensor(M[5], M[5], adj[:], ALU.subtract))
            ask(V.scalar_tensor_tensor(out=M[6], in0=M[5], scalar=S(7), in1=M[4], op0=ALU.mult, op1=ALU.mult))
            op(V.tensor_tensor(Lap[:], M[6], B[3], ALU.add))
            op(V.tensor_scalar(Lap[:], Lap[:], 0.5, None, ALU.mult))
            op(V.tensor_tensor(ident[:, N:N + 1], Lap[:, 0:1], below[:, 0:1], ALU.mult))
            V.tensor_copy(A[:], Lap[:]).then_inc(a_ready, 1)
            V.tensor_copy(sc[:, 40:41], sc[:, 1:2]).then_inc(x_ready, 1)

            SGN, DEN, HH, K2, NHU, NHW, WC, T1, T2, NHB, NHUM, ACOL, V1, VB = range(10, 24)
            h = Tally(hv)

            def step(ins):
                h.did(ins)
                return h.n

            def x_statistics(b):
                if b % (BATCH // X_CHUNKS) == 0:
                    dve.wait_ge(x_in[b // (BATCH // X_CHUNKS)], 16)
                V.bn_stats(stats[:, b, :], X[:, b, :]).then_inc(bn_done, 1)

            def second_update(k, n_first, n_scale):
                dve.wait_ge(hv, max(n_first, n_scale))
                V.scalar_tensor_tensor(out=A[:], in0=uB[:, k % 2], scalar=S(NHW), in1=A[:],
                                       op0=ALU.mult, op1=ALU.add).then_inc(a_ready, 1)

            def householder(k, pending):
                nxt = slice(k + 1, k + 2)
                uk = uB[:, k % 2]
                e_k, nh = eB[:, k:k + 1], hB[:, k:k + 1]
                if k >= BN_LAG:
                    x_statistics(k - BN_LAG)
                dve.wait_ge(sigma_ready, k + 1)
                V.tensor_scalar(S(SGN), banks[0][:, nxt], 0.0, 2.0, ALU.is_ge, ALU.mult).then_inc(sign_ready, 1)
                if pending:
                    second_update(k - 1, *pending)
                dve.wait_ge(sign_ready, k + 1)
                n_e = step(V.tensor_scalar(e_k, S(SGN), 1.0, S(0), ALU.subtract, ALU.mult))
                dve.wait_ge(hv, n_e)
                if k:
                    dve.wait_ge(um_kept, k)
                V.scalar_tensor_tensor(out=u_c[:], in0=ident[:, nxt], scalar=e_k, in1=ident[:, N:N + 1],
                                       op0=ALU.mult, op1=ALU.add).then_inc(u_ready, 1)
                dve.wait_ge(row_ready, k + 1)
                n_den = step(V.scalar_tensor_tensor(out=S(DEN), in0=uk[:, nxt], scalar=e_k, in1=banks[0][:, N:N + 1],
                                                    op0=ALU.mult, op1=ALU.add))
                dve.wait_ge(hv, n_den)
                n_u = step(V.tensor_tensor(uk[:, nxt], uk[:, nxt], e_k, ALU.add))
                n_neg = step(V.tensor_scalar(S(DEN), S(DEN), TINY, -1.0, ALU.add, ALU.mult))
                dve.wait_ge(a_ready, k + 1)
                step(V.tensor_tensor(S(ACOL), A[:, nxt], below[:, nxt], ALU.mult))
                dve.wait_ge(hv, n_neg)
                n_h = step(V.reciprocal(nh, S(DEN)))
                dve.wait_ge(hv, n_h)
                dve.wait_ge(u_ready, k + 1)
                n_hb = step(V.tensor_tensor(S(NHB), nh, below[:, nxt], ALU.mult))
                step(V.tensor_scalar(S(HH), nh, 0.5, None, ALU.mult))
                step(V.tensor_tensor(S(NHU), u_c[:], nh, ALU.mult))
                dve.wait_ge(hv, n_hb)
                n_hum = step(V.tensor_tensor(S(NHUM), u_c[:], S(NHB), ALU.mult))
                n_v1 = step(V.tensor_tensor(S(V1), uk[:, nxt], S(NHB), ALU.mult))
                dve.wait_ge(hv, n_hum)
                n_vb = step(V.tensor_scalar(S(VB), S(NHUM), uk[:, nxt], 2.0, ALU.mult, ALU.mult))
                dve.wait_ge(pb_ready, k + 1)
                dve.wait_ge(hv, n_v1)
                n_t1 = step(V.scalar_tensor_tensor(out=S(T1), in0=S(NHUM), scalar=B[1][:, nxt], in1=S(ACOL),
                                                   op0=ALU.mult, op1=ALU.add))
                n_k = step(V.tensor_tensor_reduce(out=wB[:], in0=B[1], in1=uk, scale=S(HH), scalar=0.0,
                                                  op0=ALU.mult, op1=ALU.add, accum_out=S(K2)))
                dve.wait_ge(p_ready, k + 1)
                dve.wait_ge(hv, n_t1)
                n_t2 = step(V.scalar_tensor_tensor(out=S(T2), in0=banks[2][:, 0:1], scalar=S(V1), in1=S(T1),
                                                   op0=ALU.mult, op1=ALU.add))
                dve.wait_ge(hv, n_t2)
                V.scalar_tensor_tensor(out=ident[:, N:N + 1], in0=S(VB), scalar=S(K2), in1=S(T2),
                                       op0=ALU.mult, op1=ALU.add).then_inc(x_ready, 1)
                n_wc = step(V.scalar_tensor_tensor(out=S(WC), in0=u_c[:], scalar=S(K2), in1=banks[2][:, 0:1],
                                                   op0=ALU.mult, op1=ALU.add))
                n_wb = step(V.scalar_tensor_tensor(out=wB[:], in0=uk, scalar=S(K2), in1=B[1],
                                                   op0=ALU.mult, op1=ALU.add))
                dve.wait_ge(hv, n_wc)
                n_nhw = step(V.tensor_tensor(S(NHW), S(WC), nh, ALU.mult))
                dve.wait_ge(hv, n_wb)
                n_a = step(V.scalar_tensor_tensor(out=A[:], in0=wB[:], scalar=S(NHU), in1=A[:],
                                                  op0=ALU.mult, op1=ALU.add))
                return n_a, n_nhw

            pending = None
            for k in range(LEAF):
                pending = householder(k, pending)
            second_update(LEAF - 1, *pending)
            dve.wait_ge(a_ready, LEAF + 1)
            dve.wait_ge(x_ready, LEAF + 1)
            ask(V.tensor_tensor(M[2], A[:], I, ALU.mult))
            op(V.tensor_copy(d16, banks[3][:, 0:LEAF]))
            op(V.tensor_tensor(e16, eB[:, 0:LEAF], eB[:, 0:LEAF], ALU.mult))
            op(V.memset(e16[:, LEAF - 1:LEAF], 0.0))
            op(V.scalar_tensor_tensor(out=S(8), in0=eB[:, LEAF - 1:LEAF], scalar=-1.0, in1=eB[:, LEAF - 1:LEAF],
                                      op0=ALU.mult, op1=ALU.max))
            V.tensor_tensor(d16[:, LEAF - 1:LEAF], d16[:, LEAF - 1:LEAF], S(8), ALU.subtract).then_inc(leaf_ready, 1)
            pending = None
            for k in range(LEAF, STEPS):
                pending = householder(k, pending)
            second_update(STEPS - 1, *pending)
            dve.wait_ge(a_ready, N)
            dve.wait_ge(um_kept, STEPS)

            for b in range(STEPS - BN_LAG, BATCH):
                x_statistics(b)
            dve.wait_ge(bn_done, BATCH)

            def deviations(n):
                st = stats[:].rearrange("p b s -> p s b")
                mean, var, inv, off = (ln[:, c, :] for c in range(4))
                op(V.tensor_tensor(mean, st[:, 1, :], st[:, 4, :], ALU.subtract))
                op(V.tensor_tensor(off, mean, mean, ALU.mult))
                op(V.tensor_tensor(var, st[:, 2, :], st[:, 5, :], ALU.add))
                op(V.scalar_tensor_tensor(out=var, in0=off, scalar=D / 4.0, in1=var, op0=ALU.mult, op1=ALU.add))
                op(V.tensor_tensor(mean, st[:, 1, :], st[:, 4, :], ALU.add))
                V.tensor_scalar(var, var, 1.0 / D, LN_EPS, ALU.mult, ALU.add).then_inc(ln_var, 1)
                dve.wait_ge(ln_var, n)
                dve.wait_ge(ln_dev, n)
                op(V.reciprocal(inv, inv))
                op(V.tensor_tensor(off, inv, inv, ALU.mult))
                op(V.tensor_tensor(off, off, var, ALU.mult))
                op(V.tensor_scalar(off, off, -0.5, 1.5, ALU.mult, ALU.add))
                op(V.tensor_tensor(inv, off, inv, ALU.mult))
                V.scalar_tensor_tensor(out=off, in0=mean, scalar=-0.5, in1=inv, op0=ALU.mult, op1=ALU.mult)\
                    .then_inc(ln_done, 1)

            ask(V.tensor_tensor(M[2], A[:], I, ALU.mult))
            op(V.tensor_copy(dB[:], B[3]))
            op(V.tensor_tensor(M[1], B[4], below[:, 0:N], ALU.mult))
            ask(V.tensor_tensor(M[1], M[1], hB[:], ALU.mult))
            op(V.tensor_copy(M[0], B[3]))
            op(V.tensor_copy(M[8], B[4]))
            ask(V.tensor_tensor(M[6], I, M[0], ALU.add))
            for r in range(6):
                op(V.tensor_copy(M[3], B[3]))
                ask(V.tensor_copy(M[4], B[4]))
                op(V.tensor_tensor(M[6], M[6], B[5], ALU.add))
            ask(V.tensor_tensor(M[7], M[6], hB[:], ALU.mult))
            ask(V.tensor_copy(M[5], B[3]))
            op(V.tensor_tensor(QT[:], I, B[3], ALU.add))

            deviations(1)

            LO, HI, H1, H2, LAM = 18, 19, 33, 34, 35
            op(V.scalar_tensor_tensor(out=M[0], in0=eB[:], scalar=-1.0, in1=eB[:], op0=ALU.mult, op1=ALU.max))
            op(V.tensor_copy(M[1], M[0]))
            op(V.tensor_tensor(M[1][:, 1:N], M[1][:, 1:N], M[0][:, 0:N - 1], ALU.add))
            op(V.tensor_tensor(M[3], dB[:], M[1], ALU.subtract))
            op(V.tensor_reduce(S(LO), M[3], AX_X, ALU.min))
            op(V.tensor_tensor(M[3], dB[:], M[1], ALU.add))
            op(V.tensor_reduce(S(HI), M[3], AX_X, ALU.max))
            op(V.tensor_scalar(S(H1), S(HI), S(LO), 1.001 / (N * F), ALU.subtract, ALU.mult))
            op(V.scalar_tensor_tensor(out=S(LO), in0=S(H1), scalar=-0.5, in1=S(LO), op0=ALU.mult, op1=ALU.add))
            op(V.tensor_tensor(M[2], eB[:], eB[:], ALU.mult))
            op(V.tensor_scalar(M[2], M[2], TINY, -1.0, ALU.max, ALU.mult))
            pivots = PV[:, 0:N * F]
            PV3 = pivots.rearrange("p (i f) -> p i f", f=F)

            def sturm(sem):
                op(V.tensor_tensor(PV3, dB[:].unsqueeze(2).to_broadcast([N, N, F]),
                                   XG[:].unsqueeze(1).to_broadcast([N, N, F]), ALU.subtract))
                s = Tally(sem)
                ends = [(r32, range(0, TWIST), 1), (r32b, range(N - 1, TWIST, -1), -1)]
                told = [0, 0]
                for n in range(TWIST):
                    for e, (r, rows, _) in enumerate(ends):
                        if n < len(rows):
                            if n:
                                dve.wait_ge(sem, told[e])
                            told[e] = s.did(V.reciprocal(r[:], PV3[:, rows[n], :]))
                    for e, (r, rows, way) in enumerate(ends):
                        if n < len(rows):
                            i = rows[n]
                            if i + way == TWIST and e == 0:
                                dve.wait_ge(sem, s.n)
                            else:
                                dve.wait_ge(sem, told[e])
                            told[e] = s.did(V.scalar_tensor_tensor(
                                out=PV3[:, i + way, :], in0=r[:], scalar=M[2][:, min(i, i + way):min(i, i + way) + 1],
                                in1=PV3[:, i + way, :], op0=ALU.mult, op1=ALU.add))
                s.last(dve)
                op(V.tensor_scalar(pivots, pivots, 0.0, None, ALU.is_lt))
                op(V.tensor_reduce(cnt[:], pivots.rearrange("p (i f) -> p f i", f=F), AX_X, ALU.add))

            op(V.tensor_scalar(XG[:], grid[:], S(H1), S(LO), ALU.mult, ALU.add))
            sturm(st1)
            for f in range(F):
                V.tensor_scalar(BIG[:, f * N:(f + 1) * N], iota_f[:], cnt[:, f:f + 1], None, ALU.is_ge).then_inc(stv, 1)
            answered[0] += 1
            dve.wait_ge(from_pe, answered[0])
            op(V.tensor_scalar(S(LAM), banks[6][:, 0:1], 1.0, S(H1), ALU.subtract, ALU.mult))
            op(V.tensor_tensor(S(LAM), S(LAM), S(LO), ALU.add))
            op(V.tensor_scalar(S(H2), S(H1), 1.0 / F, None, ALU.mult))
            op(V.tensor_scalar(XG[:], iota_f[:, 0:F], S(H2), S(LAM), ALU.mult, ALU.add))
            sturm(st2)
            op(V.tensor_scalar(cnt[:], cnt[:], iota_p[:], None, ALU.is_le))
            op(V.tensor_reduce(S(9), cnt[:], AX_X, ALU.add))
            op(V.tensor_scalar(S(9), S(9), 0.5, S(H2), ALU.subtract, ALU.mult))
            op(V.tensor_tensor(S(LAM), S(LAM), S(9), ALU.add))

            for l in range(LEVELS):
                op(V.tensor_copy(D4[:, l, :], dB[:] if l == 0 else D4[:, l - 1, :]))
                op(V.tensor_copy(EV[:, l, :], eB[:] if l == 0 else EV[:, l - 1, :]))
                op(V.tensor_copy(lam4[:, l:l + 1], S(LAM)))
                for c in (SPLITS[l - 1] if l else []):
                    op(V.tensor_scalar(D4[:, l, c - 1:c + 1], D4[:, l, c - 1:c + 1], M[0][:, c - 1:c], None,
                                       ALU.subtract))
                    op(V.memset(EV[:, l, c - 1:c], 0.0))
            op(V.memset(wrow[:], 0.0))
            for l in range(3):
                for c in SPLITS[l]:
                    op(V.memset(wrow[:, l, c - 1:c], 1.0))
                    op(V.tensor_scalar(wrow[:, l, c:c + 1], eB[:, c - 1:c], 0.0, -2.0, ALU.is_ge, ALU.mult))
                    op(V.tensor_scalar(wrow[:, l, c:c + 1], wrow[:, l, c:c + 1], 1.0, None, ALU.add))
                    op(V.tensor_scalar(wrow[:, 3 + l, c - 1:c + 1], M[0][:, c - 1:c].to_broadcast([N, 2]), 2.0 ** 0.5,
                                       None, ALU.mult))
            DM3 = PV[:, 0:N * LANES].rearrange("p (i l) -> p i l", l=LANES)
            RC3 = RC[:].rearrange("p (i l) -> p i l", l=LANES)

            def twisted(sem, vectors):
                for l in range(LEVELS):
                    op(V.tensor_scalar(DM3[:, :, l], D4[:, l, :], lam4[:, l:l + 1], None, ALU.subtract))
                    op(V.tensor_scalar(DM3[:, :, LEVELS + l], D4[:, l, :][:, ::-1], lam4[:, l:l + 1], None,
                                       ALU.subtract))
                s = Tally(sem)
                split_at = {c: l for l, cuts in enumerate(SPLITS) for c in cuts}
                for i in range(1, N):
                    last, at = (i - 1) * LANES, i * LANES
                    for lane in (0, LEVELS):
                        if i > 1:
                            dve.wait_ge(sem, s.n - 1)
                        s.did(V.reciprocal(RC[:, last + lane:last + lane + LEVELS],
                                           PV[:, last + lane:last + lane + LEVELS]))
                    for lane, row in ((0, i - 1), (LEVELS, N - 1 - i)):
                        live = split_at.get(row + 1, LEVELS - 1) + 1
                        nx = PV[:, at + lane:at + lane + live]
                        dve.wait_ge(sem, s.n - 1)
                        s.did(V.scalar_tensor_tensor(out=nx, in0=RC[:, last + lane:last + lane + live],
                                                     scalar=M[2][:, row:row + 1], in1=nx, op0=ALU.mult, op1=ALU.add))
                s.last(dve)
                op(V.reciprocal(RC[:, (N - 1) * LANES:], PV[:, (N - 1) * LANES:N * LANES]))
                op(V.tensor_scalar(RC[:], RC[:], 1e15, -1e15, ALU.min, ALU.max))
                for l in range(LEVELS):
                    qf, qb = DM3[:, :, l], DM3[:, :, LEVELS + l][:, ::-1]
                    rf, rb = RC3[:, :, l], RC3[:, :, LEVELS + l][:, ::-1]
                    op(V.scalar_tensor_tensor(out=M[3], in0=qb, scalar=lam4[:, l:l + 1], in1=qf,
                                              op0=ALU.add, op1=ALU.add))
                    op(V.tensor_tensor(M[3], M[3], D4[:, l, :], ALU.subtract))
                    op(V.scalar_tensor_tensor(out=M[4], in0=M[3], scalar=-1.0, in1=M[3], op0=ALU.mult, op1=ALU.max))
                    op(V.tensor_reduce(S(9), M[4], AX_X, ALU.min))
                    op(V.tensor_scalar(M[4], M[4], S(9), None, ALU.is_le))
                    total(S(9), M[3], M[4])
                    op(V.memset(M[5][:, 0:1], 0.0))
                    op(V.tensor_tensor(M[5][:, 1:N], EV[:, l, 0:N - 1], rb[:, 1:N], ALU.mult))
                    op(V.tensor_tensor_scan(M[6], M[5], M[4], 0.0, ALU.mult, ALU.add))
                    op(V.tensor_tensor(M[5], EV[:, l, :], rf, ALU.mult))
                    op(V.tensor_tensor_scan(M[7][:, ::-1], M[5][:, ::-1], M[4][:, ::-1], 0.0, ALU.mult, ALU.add))
                    op(V.tensor_tensor(M[6], M[6], M[7], ALU.add))
                    op(V.tensor_tensor(V4[:, l, :], M[6], M[4], ALU.subtract))
                    total(S(20 + l), V4[:, l, :], V4[:, l, :])
                    if not vectors:
                        op(V.reciprocal(S(29), S(20 + l)))
                        op(V.tensor_tensor(S(9), S(9), S(29), ALU.mult))
                        op(V.tensor_scalar(S(9), S(9), RAYLEIGH_CLIP, -RAYLEIGH_CLIP, ALU.min, ALU.max))
                        op(V.tensor_tensor(lam4[:, l:l + 1], lam4[:, l:l + 1], S(9), ALU.add))

            twisted(tw1, False)
            twisted(tw2, True)
            V.tensor_copy(S(41), S(20)).then_inc(rs_in, 1)
            dve.wait_ge(rs_out, 2)
            op(V.reciprocal(S(24, 4), S(24, 4)))
            for l in range(LEVELS):
                op(V.tensor_scalar(V4[:, l, :], V4[:, l, :], S(24 + l), None, ALU.mult))
            op(V.tensor_tensor(S(30), lam4[:, 0:1], ident[:, N - 1:N], ALU.mult))
            op(V.scalar_tensor_tensor(out=S(31), in0=ident[:, 64:65], scalar=wrow[:, 0, 64:65], in1=ident[:, 63:64],
                                      op0=ALU.mult, op1=ALU.add))
            ask(V.tensor_copy(S(42), S(30)))
            op(V.tensor_scalar(S(43), banks[6][:, 0:1], DEFLATE, None, ALU.mult))
            CC, ZZ, LF = 44, 47, 50
            for l in range(3):
                total(S(CC + l), V4[:, 0, :], wrow[:, l, :])
                op(V.scalar_tensor_tensor(out=M[3], in0=V4[:, l + 1, :], scalar=-1.0, in1=V4[:, l + 1, :],
                                          op0=ALU.mult, op1=ALU.max))
                total(S(ZZ + l), M[3], wrow[:, 3 + l, :])
                op(V.tensor_scalar(S(ZZ + l), S(ZZ + l), S(43), None, ALU.is_le))
            dve.wait_ge(leaf_sign, 1)
            op(V.tensor_scalar(S(LF), V4[:, 0, 0:1], sg[:, 0:1], -1.0, ALU.mult, ALU.mult))
            op(V.tensor_scalar(S(CC, 3), S(CC, 3), 0.0, None, ALU.is_lt))
            op(V.tensor_scalar(S(LF), S(LF), 0.0, None, ALU.is_lt))
            for l in (2, 1, 0):
                op(V.tensor_tensor(S(LF), S(LF), S(CC + l), ALU.subtract))
                op(V.scalar_tensor_tensor(out=S(LF), in0=S(LF), scalar=S(ZZ + l), in1=S(CC + l),
                                          op0=ALU.mult, op1=ALU.add))

            ask(V.tensor_copy(M[1], B[3]))
            op(V.tensor_copy(UT[:], B[3]))
            op(V.tensor_copy(S(32), banks[5][:, 0:1]))
            ask(V.tensor_copy(U[:], B[4]))
            for r in range(REFINES):
                if r:
                    ask(V.tensor_tensor(U[:], U[:], B[3], ALU.add))
                ask(V.tensor_copy(M[0], B[3]))
                op(V.tensor_copy(M[1], B[4]))
                op(V.tensor_copy(M[2], B[5]))
                total(S(51), M[1], I)
                total(S(52), M[2], I)
                op(V.reciprocal(S(52), S(52)))
                op(V.tensor_tensor(S(51), S(51), S(52), ALU.mult))
                ask(V.tensor_scalar(M[5], I, S(51), None, ALU.mult))
                op(V.tensor_scalar(M[3], B[6], S(51), None, ALU.subtract))
                op(V.tensor_tensor(M[4], I, M[2], ALU.subtract))
                op(V.tensor_tensor(M[6], M[4], B[6], ALU.mult))
                op(V.tensor_tensor(M[6], M[6], M[1], ALU.add))
                op(V.tensor_tensor(M[6], M[6], M[3], ALU.mult))
                op(V.scalar_tensor_tensor(out=M[6], in0=M[4], scalar=0.5 * REGULAR, in1=M[6],
                                          op0=ALU.mult, op1=ALU.add))
                op(V.tensor_tensor(M[3], M[3], M[3], ALU.mult))
                op(V.tensor_scalar(M[3], M[3], REGULAR, None, ALU.add))
                op(V.reciprocal(M[3], M[3]))
                ask(V.tensor_tensor(M[5], M[6], M[3], ALU.mult))
                op(V.tensor_tensor(UT[:], UT[:], B[4], ALU.add))
            ask(V.tensor_tensor(U[:], U[:], B[3], ALU.add))
            op(V.tensor_copy(S(53), banks[3][:, 0:1]))
            op(V.tensor_scalar(S(54), S(53), 0.0, None, ALU.is_lt))
            op(V.tensor_tensor(S(55), S(53), S(53), ALU.mult))
            op(V.tensor_scalar(S(55), S(55), 1e-8, None, ALU.is_gt))
            op(V.tensor_tensor(S(54), S(54), S(LF), ALU.subtract))
            op(V.scalar_tensor_tensor(out=S(54), in0=S(54), scalar=S(55), in1=S(LF), op0=ALU.mult, op1=ALU.add))
            op(V.tensor_scalar(S(54), S(54), 2.0, -1.0, ALU.mult, ALU.add))
            ask(V.tensor_scalar(UT[:], UT[:], S(54), None, ALU.mult))
            V.tensor_copy(U[:], B[4]).then_inc(eig_done, 1)
            dve.wait_ge(eig_done, 1)
            dve.wait_ge(w_kept, 2 * SKIPS + 3)

            def group(it, i):
                return bass.ds(it * (STREAMS * GB) + i * GB, GB)

            def statistics(it, i):
                dve.wait_ge(x1_ready[i], it + 1)
                for b in range(GB):
                    at = bass.ds(it * (STREAMS * GB) + (i * GB + b), 1)
                    V.bn_stats(stats[:, at, :].rearrange("p b s -> p (b s)"),
                               X[:, at, :].rearrange("p b d -> p (b d)")).then_inc(bn_done, 1)

            def first_layer(it, before):
                for i in range(STREAMS):
                    dve.wait_ge(agg_ready[i], it + 1)
                    V.tensor_copy(mixS[i], bank[i][0]).then_inc(agg_kept[i], 1)
                if before is not None:
                    statistics(before, 0)
                    statistics(before, 1)
                for i in range(STREAMS):
                    dve.wait_ge(out_ready[i], it + 1)
                    V.tensor_tensor(batches(zS[i]), batches(bank[i][2]), b2B[:].unsqueeze(1).to_broadcast([N, GB, D]),
                                    ALU.add).then_inc(out_kept[i], 1)
                if before is not None:
                    statistics(before, 2)
                    statistics(before, 3)
                for i in range(STREAMS):
                    dve.wait_ge(back_ready[i], it + 1)
                    V.tensor_tensor(X[:, group(it, i), :], X[:, group(it, i), :], batches(bank[i][3]),
                                    ALU.add).then_inc(x1_ready[i], 1)

            first_layer(0, None)
            with V.Fori(1, ROUNDS) as it:
                first_layer(it, it - 1)
            for i in range(STREAMS):
                statistics(ROUNDS - 1, i)
            dve.wait_ge(bn_done, 2 * BATCH)
            deviations(2)

            def cell(it, c, i):
                p, j, _, nb = CELLS[c]
                T = nb * (N // p)
                dve.wait_ge(acts_ready[i], it * len(CELLS) + c + 1)
                if j == 0:
                    V.tensor_tensor(cS[i][:, 0:T], gI[i][:, 0:T], gG[i][:, 0:T], ALU.mult).then_inc(cell_ready[i], 1)
                    return
                parts = it * PARTS + sum(2 for _, jj, _, _ in CELLS[:c] if jj)
                V.tensor_tensor(gI[i][:, 0:T], gI[i][:, 0:T], gG[i][:, 0:T], ALU.mult).then_inc(cell_part[i], 1)
                V.tensor_tensor(gF[i][:, 0:T], gF[i][:, 0:T], cS[i][:, 0:T], ALU.mult).then_inc(cell_part[i], 1)
                dve.wait_ge(cell_part[i], parts + 2)
                V.tensor_tensor(cS[i][:, 0:T], gI[i][:, 0:T], gF[i][:, 0:T], ALU.add).then_inc(cell_ready[i], 1)

            def hidden(it, c, i):
                p, j, b0, nb = CELLS[c]
                W = N // p

                def by_batch(v):
                    return v[:, 0:nb * W].rearrange("p (b w) -> p b w", b=nb)

                dve.wait_ge(tanh_ready[i], it * len(CELLS) + c + 1)
                dst = by_batch(hS[i]) if j < p - 1 else batches(HS[i])[:, b0:b0 + nb, p - 1:W * p:p]
                V.tensor_tensor(dst, by_batch(gO[i]), by_batch(tS[i]), ALU.mult).then_inc(hidden_ready[i], 1)

            def keep_mix(it, i):
                dve.wait_ge(mix_ready[i], it + 1)
                V.tensor_copy(mixS[i], bank[i][0]).then_inc(mix_kept[i], 1)

            def residual(it, i):
                dve.wait_ge(turned_ready[i], it + 1)
                V.tensor_tensor(X[:, group(it, i), :], X[:, group(it, i), :], batches(bank[i][1]),
                                ALU.add).then_inc(sum_ready[i], 1)

            def second_layer(it):
                for i in range(STREAMS):
                    dve.wait_ge(lin_ready[i], it + 1)
                    V.tensor_tensor(batches(linS[i]), batches(bank[i][2]), G0[:].unsqueeze(1).to_broadcast([N, GB, N]),
                                    ALU.add).then_inc(lin_kept[i], 1)
                for i in range(STREAMS):
                    dve.wait_ge(z_ready[i], it + 1)
                    V.tensor_tensor(batches(zS[i]), batches(bank[i][3]), bg1B[:].unsqueeze(1).to_broadcast([N, GB, D]),
                                    ALU.add).then_inc(z_kept[i], 1)
                for n, turn in enumerate(TURNS):
                    cell(it, *turn)
                    if n:
                        hidden(it, *TURNS[n - 1])
                hidden(it, *TURNS[-1])

            for i in range(STREAMS):
                keep_mix(0, i)
            with V.Fori(0, ROUNDS - 1) as it:
                second_layer(it)
                for i in range(STREAMS):
                    keep_mix(it + 1, i)
                    residual(it, i)
            second_layer(ROUNDS - 1)
            for i in range(STREAMS):
                residual(ROUNDS - 1, i)


_INS = ['x', 'adj', 'L0_gnn_W1', 'L0_gnn_b1', 'L0_gnn_W2', 'L0_gnn_b2', 'L1_gnn_Wg0', 'L1_gnn_bg0', 'L1_gnn_Wg1',
        'L1_gnn_bg1', 'L1_gnn_Wih', 'L1_gnn_Whh', 'L1_gnn_bih', 'L1_gnn_bhh']
_OUTS = [((BATCH, N, D), 'float32')]


def kernel(**inputs):
    import numpy as _np
    import concourse.bacc as _bacc
    from concourse import mybir as _mybir
    from concourse.bass_utils import run_bass_kernel_spmd as _run

    nc = _bacc.Bacc("TRN2", target_bir_lowering=False, num_devices=1)
    arrays, args = {}, {}
    for name in _INS:
        a = _np.ascontiguousarray(inputs[name])
        arrays[f"in_{name}"] = a
        args[name] = nc.dram_tensor(f"in_{name}", a.shape, _mybir.dt.from_np(a.dtype), kind="ExternalInput").ap()
    o = nc.dram_tensor("out_0", _OUTS[0][0], F32, kind="ExternalOutput").ap()
    build(nc, args, o)
    r = _run(nc, [arrays], core_ids=[0])
    return r.results[0]["out_0"]
```
